# Optimizing a Trainium2 kernel written in Bass

```python
import numpy as np
import jax
import jax.numpy as jnp

def _softmax(x, axis=-1):
    return jax.nn.softmax(x, axis=axis)

def _gelu(x):
    return jax.nn.gelu(x, approximate=True)

def _silu(x):
    return jax.nn.silu(x)

def _sigmoid(x):
    return jax.nn.sigmoid(x)

def _layernorm(x, axis=-1, eps=1e-05):
    m = jnp.mean(x, axis=axis, keepdims=True)
    v = jnp.var(x, axis=axis, keepdims=True)
    return (x - m) / jnp.sqrt(v + eps)

def _scatter_add(tgt, idx, src, axis=0):
    return tgt.at[idx].add(src)

def _segment_sum(src, seg, n):
    return jax.ops.segment_sum(src, seg, n)
kernel_name = 'mk_adaln_d1_jaxref_r8_09cd5b'

def setup_inputs(seed: int=0):
    np.random.seed(seed)
    _w = jnp.asarray

    def _L0_attn_setup():
        import jax, jax.numpy as jnp
        import numpy as np
        D = 128
        key = jax.random.key(seed)
        ks = jax.random.split(key, 7)
        s = 1.0 / np.sqrt(D)
        return {'x': jax.random.normal(ks[0], (4, 256, D), dtype=jnp.float32), 'Wq': jax.random.uniform(ks[1], (D, D), jnp.float32, -s, s), 'bq': jax.random.uniform(ks[2], (D,), jnp.float32, -s, s), 'Wk': jax.random.uniform(ks[3], (D, D), jnp.float32, -s, s), 'bk': jax.random.uniform(ks[4], (D,), jnp.float32, -s, s), 'Wv': jax.random.uniform(ks[5], (D, D), jnp.float32, -s, s), 'bv': jax.random.uniform(ks[6], (D,), jnp.float32, -s, s)}
    _L0_attn_in = _L0_attn_setup()

    def _L0_ffn_setup():
        import jax, jax.numpy as jnp
        import numpy as np
        EMBED_DIM = 128
        HIDDEN_DIM = 512
        NUM_EXPERTS = 8
        TOP_K = 2
        key = jax.random.key(seed)
        ks = jax.random.split(key, 4)
        std1 = float(np.sqrt(2.0 / EMBED_DIM))
        std2 = float(np.sqrt(2.0 / HIDDEN_DIM))
        x = jax.random.normal(ks[0], (1, 256, EMBED_DIM), dtype=jnp.float32)
        w_router = jax.random.normal(ks[1], (EMBED_DIM, NUM_EXPERTS), dtype=jnp.float32) * 0.02
        w1 = jax.random.normal(ks[2], (NUM_EXPERTS, EMBED_DIM, HIDDEN_DIM), dtype=jnp.float32) * std1
        b1 = jnp.zeros((NUM_EXPERTS, HIDDEN_DIM), dtype=jnp.float32)
        w2 = jax.random.normal(ks[3], (NUM_EXPERTS, HIDDEN_DIM, EMBED_DIM), dtype=jnp.float32) * std2
        b2 = jnp.zeros((NUM_EXPERTS, EMBED_DIM), dtype=jnp.float32)
        return {'x': x, 'w_router': w_router, 'w1': w1, 'b1': b1, 'w2': w2, 'b2': b2}
    _L0_ffn_in = _L0_ffn_setup()
    _L0_c = _w((lambda *s: np.random.randn(*s).astype(np.float32) * 0.05)(4, 128))
    _L0_wmod = _w((lambda *s: np.random.randn(*s).astype(np.float32) * 0.05)(128, 6 * 128) * 128 ** (-0.5))
    _d = {'L0_attn_x': _L0_attn_in['x'], 'L0_attn_Wq': _L0_attn_in['Wq'], 'L0_attn_bq': _L0_attn_in['bq'], 'L0_attn_Wk': _L0_attn_in['Wk'], 'L0_attn_bk': _L0_attn_in['bk'], 'L0_attn_Wv': _L0_attn_in['Wv'], 'L0_attn_bv': _L0_attn_in['bv'], 'L0_ffn_w_router': _L0_ffn_in['w_router'], 'L0_ffn_w1': _L0_ffn_in['w1'], 'L0_ffn_b1': _L0_ffn_in['b1'], 'L0_ffn_w2': _L0_ffn_in['w2'], 'L0_ffn_b2': _L0_ffn_in['b2'], 'L0_c': _L0_c, 'L0_wmod': _L0_wmod}
    _x0 = _d['L0_attn_x']
    _d['L0_attn_x'] = jax.random.normal(jax.random.fold_in(jax.random.key(seed), 1), (4, 1024, 128), dtype=_x0.dtype)
    del _x0
    return _d

def reference(L0_attn_x, L0_attn_Wq, L0_attn_bq, L0_attn_Wk, L0_attn_bk, L0_attn_Wv, L0_attn_bv, L0_ffn_w_router, L0_ffn_w1, L0_ffn_b1, L0_ffn_w2, L0_ffn_b2, L0_c, L0_wmod):

    def _L0_attn_ref(x, Wq, bq, Wk, bk, Wv, bv):
        import jax, jax.numpy as jnp
        import numpy as np
        D = 128
        q = jnp.einsum('bsd,ed->bse', x, Wq) + bq
        k = jnp.einsum('bsd,ed->bse', x, Wk) + bk
        v = jnp.einsum('bsd,ed->bse', x, Wv) + bv
        scores = jnp.einsum('bqd,bkd->bqk', q, k)
        attn = jax.nn.softmax(scores, axis=-1)
        return jnp.einsum('bqk,bkd->bqd', attn, v)

    def _L0_ffn_ref(x, w_router, w1, b1, w2, b2):
        import jax, jax.numpy as jnp
        import numpy as np
        EMBED_DIM = 128
        HIDDEN_DIM = 512
        NUM_EXPERTS = 8
        TOP_K = 2
        orig_shape = x.shape
        xf = x.reshape(-1, EMBED_DIM)
        logits = xf @ w_router
        probs = jax.nn.softmax(logits, axis=-1)
        topk_w, topk_idx = jax.lax.top_k(probs, TOP_K)
        mask = jax.nn.one_hot(topk_idx, NUM_EXPERTS, dtype=xf.dtype)
        weights = jnp.sum(topk_w[..., None] * mask, axis=1)
        h = jnp.einsum('te,ieh->tih', xf, w1) + b1
        h = jax.nn.gelu(h)
        out = jnp.einsum('tih,ihe->tie', h, w2) + b2
        out = jnp.sum(out * weights[..., None], axis=1)
        return out.reshape(orig_shape)
    x = L0_attn_x
    mod = (_silu(L0_c) @ L0_wmod).reshape(L0_c.shape[0], 6, 1, -1)
    sa, ca, ga, sb, cb, gb = (mod[:, 0], mod[:, 1], mod[:, 2], mod[:, 3], mod[:, 4], mod[:, 5])
    ga = (2 * (ga >= 0) - 1) * jnp.maximum(jnp.abs(ga), 0.25)
    gb = (2 * (gb >= 0) - 1) * jnp.maximum(jnp.abs(gb), 0.25)
    h = _layernorm(x, axis=-1) * (1 + ca) + sa
    x = x + ga * _L0_attn_ref(h, L0_attn_Wq, L0_attn_bq, L0_attn_Wk, L0_attn_bk, L0_attn_Wv, L0_attn_bv)
    h = _layernorm(x, axis=-1) * (1 + cb) + sb
    x = x + gb * _L0_ffn_ref(h, L0_ffn_w_router, L0_ffn_w1, L0_ffn_b1, L0_ffn_w2, L0_ffn_b2)
    return x

_drawn_inputs = setup_inputs


def setup_inputs(seed=0):
    import zlib

    import numpy as np

    out = dict(_drawn_inputs(seed))
    spreads = {'L0_ffn_b1': (0.0, 0.8), 'L0_ffn_b2': (0.0, 0.8)}
    factors = {'L0_attn_bq': 3.924, 'L0_attn_bk': 8.0, 'L0_attn_bv': 3.66}
    for name, (base, spread) in spreads.items():
        noise = np.random.default_rng([zlib.crc32(name.encode()), seed]).standard_normal(out[name].shape)
        drawn = base * np.exp(spread * noise) if base else spread * noise
        out[name] = jnp.asarray(drawn.astype(out[name].dtype))
    for name, factor in factors.items():
        out[name] = (out[name] * factor).astype(out[name].dtype)
    return out
```

```python
from contextlib import ExitStack

import concourse.bass as bass
from concourse import mybir

ALU = mybir.AluOpType
ACT = mybir.ActivationFunctionType
AX = mybir.AxisListType
F32 = mybir.dt.float32
F32R = mybir.dt.float32r
I32 = mybir.dt.int32
U32 = mybir.dt.uint32

P = 128
D = 128
B = 4
SEQ = 1024
TPB = SEQ // P
NT = B * TPB
GQ = 4
NG = NT // GQ
E = 8
HID = 512
HB = HID // P
TOPK = 2
HALVES = 2
HT = NT // HALVES
TILES = (HT * P * TOPK + E * (P - 1)) // P
TILES += TILES % 2
ROW = D + 2
PAIRS = NT * P * TOPK
NSLOT = HALVES * TILES * P
EPS = 1e-5
THR = HT



def earlier(p, u, d):
    return p + (u - d) // 2, (u - d) % 2


ROUNDS_A = {2: ("P", 0), 3: ("P", 2), 4: ("P", 3), 5: ("P", 4), 6: ("P", 5), 7: ("P", 7)}
ROUNDS_B = {0: ("G", 2), 1: ("G", 0), 2: ("P", 1), 3: ("G", 1), 4: ("G", 2), 5: ("G", 0), 6: ("P", 6), 7: ("G", 1)}
STEPS = NT + 9
ROUTE0 = HT + 8


def rounds_of(i, where):
    r = (ROUNDS_A if where == "a" else ROUNDS_B).get(i % TPB)
    if r is None:
        return None
    kind, n = r
    if kind == "P":
        b = i // TPB + 1
        return ("P", b, n) if b < B else None
    last = {0: 9, 1: 11, 2: 12}[n]
    if (i - last) % GQ or i < last:
        return None
    g = (i - last) // GQ
    return ("G", g, n) if g < NG else None


def all_rounds():
    order = [("P", 0, n) for n in range(8)]
    for i in range(STEPS):
        order += [r for r in (rounds_of(i, "a"), rounds_of(i, "b")) if r]
    return order


def build(nc, x, Wq, bq, Wk, bk, Wv, bv, w_router, w1, b1, w2, b2, c, wmod, out):
    ORDER = all_rounds()
    NTH = {r: n for n, r in enumerate(ORDER)}

    with ExitStack() as ctx:
        def sb(name, shape, dt=F32):
            return ctx.enter_context(nc.sbuf_tensor(name, shape, dt))

        def sem(name):
            return ctx.enter_context(nc.semaphore(name))

        ps_s = ctx.enter_context(nc.psum_tensor("ps_s", [P, 2, SEQ], F32))
        ps_t = ctx.enter_context(nc.psum_tensor("ps_t", [P, TPB, P], F32))
        ps_o = ctx.enter_context(nc.psum_tensor("ps_o", [P, GQ * P], F32))
        ps_m = ctx.enter_context(nc.psum_tensor("ps_m", [P, GQ * P], F32))

        ident = sb("ident", [P, P])
        before = sb("before", [P, P])
        ones = sb("ones", [P, P])
        iota_e = sb("iota_e", [P, E])
        iota_t = sb("iota_t", [P, TILES])
        thr = sb("thr", [P, THR])
        keep = sb("keep", [P, E, HT])
        trash = sb("trash", [P, HALVES * TILES])
        eps_c = sb("eps_c", [P, NT])
        mhalf = sb("mhalf", [P, TPB])

        x_sb = sb("x_sb", [P, NT, D])
        wT_hi = sb("wT_hi", [P, 3, D], F32R)
        wT_lo = sb("wT_lo", [P, 3, D], F32R)
        b_cols = sb("b_cols", [P, 2])
        bv_bc = sb("bv_bc", [P, D])
        cT = sb("cT", [P, B])
        c_exp = sb("c_exp", [P, B])
        c_silu = sb("c_silu", [P, B])
        mod_a = sb("mod_a", [P, 3, B])
        sgn_a = sb("sgn_a", [P, B])
        mod_b = sb("mod_b", [P, B, 3, D])
        sgn_b = sb("sgn_b", [P, D])
        wr_sb = sb("wr_sb", [P, E])

        stats = sb("stats", [P, GQ, 6])
        mv1 = sb("mv1", [P, TPB, 2])
        mv2 = sb("mv2", [P, GQ, 2])
        var1 = sb("var1", [P, TPB])
        rstd1 = sb("rstd1", [P, TPB])
        var2 = sb("var2", [P, GQ])
        rstd2 = sb("rstd2", [P, GQ])
        h_f = sb("h_f", [P, GQ * P])
        h_hi = sb("h_hi", [P, SEQ], F32R)
        h_lo = sb("h_lo", [P, SEQ], F32R)
        q_hi = sb("q_hi", [P, 2, SEQ], F32R)
        q_lo = sb("q_lo", [P, 2, SEQ], F32R)
        k_hi = sb("k_hi", [P, 2, SEQ], F32R)
        k_lo = sb("k_lo", [P, 2, SEQ], F32R)
        v_sb = sb("v_sb", [P, 2, TPB, D])
        nmax = sb("nmax", [P, NT])
        rsum = sb("rsum", [P, NT])
        rinv = sb("rinv", [P, NT])
        probs = sb("probs", [P, 2, SEQ])
        pT = sb("pT", [P, 2, TPB, GQ * P])
        early = pT[:, 1].rearrange("p a b -> p (a b)")
        w_raw = early[:, 0:3 * D].rearrange("p (w d) -> p w d", w=3)
        wmod_sb = early[:, 3 * D:9 * D].rearrange("p (j f) -> p j f", j=6)
        c_rep = early[:, 9 * D:(9 + B) * D].rearrange("p (b f) -> p b f", b=B)
        oT = sb("oT", [P, GQ * P])
        h2 = sb("h2", [P, NT, ROW])
        h2T = sb("h2T", [P, GQ * P])
        logits = sb("logits", [P, NT, E])

        r_max = sb("r_max", [P, HT])
        r_sub = sb("r_sub", [P, HT, E])
        r_exp = sb("r_exp", [P, HT, E])
        r_sum = sb("r_sum", [P, HT])
        r_inv = sb("r_inv", [P, HT])
        r_prob = sb("r_prob", [P, HT, E])
        top_w = sb("top_w", [P, NT, 8])
        top_i = sb("top_i", [P, HT, 8], U32)
        top_f = sb("top_f", [P, HT, TOPK])
        hot = sb("hot", [P, TOPK, HT, E])
        hot2 = sb("hot2", [P, HT, E])
        totals = sb("totals", [P, E, HT])
        upto = sb("upto", [P, E, HT])
        cmp_n = sb("cmp_n", [P, E, THR])
        n_tiles = sb("n_tiles", [P, E])
        end_t = sb("end_t", [P, E])
        base_e = sb("base_e", [P, E])
        pos = sb("pos", [P, HT, E])
        pos_k = sb("pos_k", [P, TOPK, HT, E])
        slot_f = sb("slot_f", [P, TOPK, HT])
        slot_i = sb("slot_i", [P, HALVES, TOPK, HT], I32)
        cmp_t = h_f[:, 0:TILES * E].rearrange("p (t e) -> p t e", e=E)
        tile_e = sb("tile_e", [P, HALVES * TILES])
        tile_i = sb("tile_i", [P, HALVES * TILES], I32)

        w1_hl = sb("w1_hl", [P, E, 2, HID], F32R)
        w2_sb = sb("w2_sb", [P, E, HB, D])
        w1_raw = sb("w1_raw", [P, 2, HID])
        blank = sb("blank", [P, ROW])
        xs = sb("xs", [P, 2, ROW])
        xT_hi = sb("xT_hi", [P, 2, P], F32R)
        xT_lo = sb("xT_lo", [P, 2, P], F32R)
        hb = probs
        late = pT[:].rearrange("p a b c -> p (a b c)")
        gl = late[:, 0:4 * HID].rearrange("p (w u h) -> p w u h", w=2, u=2)
        b1_bc = late[:, 4 * HID:(4 + E) * HID]
        b2_bc = late[:, (4 + E) * HID:(4 + E) * HID + E * D]
        yy_bufs = late[:, 0:16 * D].rearrange("p (u t kd) -> p u t kd", u=2, t=4)
        y_sb = sb("y_sb", [P, 2, D])
        dst_f = sb("dst_f", [P, HALVES * TILES])
        dst_i = sb("dst_i", [P, 2, 1], I32)
        slots_dram = nc.dram_tensor("slots", (NSLOT, ROW), F32, kind="Internal").ap()
        y_dram = nc.dram_tensor("pairs", (PAIRS + NSLOT, D), F32, kind="Internal").ap()

        S = {n: sem(n) for n in (
            "const_ready ident_ready w_loaded x_loaded c_loaded wmod_loaded w1_loaded w2_loaded w1_split bias_loaded "
            "mod_mm mod_ready c_exp_ready c_silu_ready wT_mm wT_hi_ready wT_lo_ready "
            "ln1_stats rstd1_var z1_ready dve_chain pool_chain act_chain "
            "m_filled m_freed h_full h_hi_ready h_lo_ready qk_hi qk_lo v_ready "
            "scores max_ready exp_ready turned copied_act copied_dve pv_part o_scaled x1_ready ln2_stats h2_ready "
            "h2T_ready logits_ready route_sub route_exp route_hot route_mm route_slots route_tiles blank_ready "
            "slots_blank scattered_0 scattered_1 x_in_0 x_in_1 xT_mm xT_hi_ready xT_ready hid_mm hid_biased gelu_ready g_turned g_copied "
            "y_mm y_ready dst_ready sent y_out_0 y_out_1 y_in combined out_done").split()}

        def s(name):
            return S[name]

        x_t = x.rearrange("b (t p) d -> p (b t) d", p=P)
        out_t = out.rearrange("b (t p) d -> p (b t) d", p=P)
        y_pairs = y_dram[0:PAIRS].rearrange("(t p k) d -> p t (k d)", p=P, k=TOPK)
        block = ctx.enter_context(nc.Block())

        @block.sync
        def _(sp):
            for h, w in enumerate((Wq, Wk, Wv)):
                sp.dma_start(w_raw[:, h], w).then_inc(s("w_loaded"), 16)
            for b in range(B):
                sp.dma_start(x_sb[:, b * TPB:(b + 1) * TPB], x_t[:, b * TPB:(b + 1) * TPB]).then_inc(s("x_loaded"), 16)
                sp.wait_ge(s("x_loaded"), 16 * (b + 1))
                if b == 0:
                    sp.dma_start(wmod_sb[:], wmod.rearrange("k (j f) -> k j f", j=6)).then_inc(s("wmod_loaded"), 16)
            sp.dma_start(w2_sb[:], w2.rearrange("e (j p) d -> p e j d", p=P)).then_inc(s("w2_loaded"), 16)
            sp.wait_ge(s("blank_ready"), 1)
            n_all = HALVES * TILES
            sp.dma_start(slots_dram.rearrange("(p t) r -> p t r", p=P),
                         blank[:].rearrange("p (o r) -> p o r", o=1).to_broadcast([P, n_all, ROW])).then_inc(s("slots_blank"), 16)

            for e in range(E):
                if e >= 2:
                    sp.wait_ge(s("w1_split"), e - 1)
                if e >= 1:
                    sp.wait_ge(s("w1_loaded"), 16 * e)
                sp.dma_start(w1_raw[:, e % 2], w1[e]).then_inc(s("w1_loaded"), 16)
            sp.wait_ge(s("pv_part"), NT)
            sp.dma_start(b1_bc, b1.rearrange("(o e) h -> o (e h)", o=1).to_broadcast([P, E * HID])).then_inc(s("bias_loaded"), 16)
            sp.dma_start(b2_bc, b2.rearrange("(o e) d -> o (e d)", o=1).to_broadcast([P, E * D])).then_inc(s("bias_loaded"), 16)

            def load_tile(p, u):
                t = p * 2 + u
                if not isinstance(p, int) or t >= 2:
                    sp.wait_ge(s("xT_mm"), t - 1)
                    sp.wait_ge(s("dst_ready"), t - 1)
                sp.dma_start(xs[:, u], slots_dram[bass.ds(t * P, P)]).then_inc(s(f"x_in_{u}"), 16)

            for half in range(HALVES):
                sp.wait_ge(s(f"scattered_{half}"), 16 * TOPK * HT)
                p0 = half * TILES // 2
                load_tile(p0, 0)
                load_tile(p0, 1)
                with sp.Fori(0, TILES // 2 - 1) as j:
                    for u in range(2):
                        load_tile(j + (p0 + 1), u)
            for half in range(HALVES):
                for q in range(4):
                    n = half * 4 + q
                    a = half * HT + q * 4
                    sp.wait_ge(s("combined"), n + 1)
                    sp.dma_start(out_t[:, a:a + 4], x_sb[:, a:a + 4]).then_inc(s("out_done"), 16)
            sp.wait_ge(s("out_done"), 16 * 4 * HALVES)

        @block.gpsimd
        def _(pool):
            chain = [0]

            def link(ins):
                chain[0] += 1
                ins.then_inc(s("pool_chain"), 1)
                pool.wait_ge(s("pool_chain"), chain[0])

            nc.gpsimd.memset(ident[:], 0.0).then_inc(s("pool_chain"), 1)
            nc.gpsimd.memset(before[:], 0.0).then_inc(s("pool_chain"), 1)
            nc.gpsimd.memset(ones[:], 1.0).then_inc(s("pool_chain"), 1)
            nc.gpsimd.memset(keep[:], 1.0).then_inc(s("pool_chain"), 1)
            chain[0] = 4
            pool.wait_ge(s("pool_chain"), 4)
            nc.gpsimd.affine_select(out=ident[:], in_=ident[:], compare_op=ALU.not_equal, fill=1.0, base=0,
                                    pattern=[[-1, P]], channel_multiplier=1).then_inc(s("ident_ready"), 1)
            nc.gpsimd.affine_select(out=before[:], in_=before[:], compare_op=ALU.is_ge, fill=1.0, base=0,
                                    pattern=[[-1, P]], channel_multiplier=1)
            nc.gpsimd.memset(keep[:, :, 0:1], 0.0)
            nc.gpsimd.memset(mhalf[:], -0.5)
            f = dict(allow_small_or_imprecise_dtypes=True)
            nc.gpsimd.iota(iota_e[:], [[1, E]], base=0, channel_multiplier=0, **f)
            nc.gpsimd.iota(iota_t[:], [[1, TILES]], base=0, channel_multiplier=0, **f)
            nc.gpsimd.iota(thr[:], [[P, THR]], base=0, channel_multiplier=0, **f)
            nc.gpsimd.iota(trash[:], [[P, HALVES * TILES]], base=PAIRS, channel_multiplier=1, **f)
            nc.gpsimd.iota(h2[:, :, D:D + 1], [[TOPK * P, NT], [1, 1]], base=0, channel_multiplier=TOPK, **f)
            link(nc.gpsimd.memset(blank[:], 0.0))
            link(nc.gpsimd.memset(blank[:, D:D + 1], 1e6))
            nc.gpsimd.memset(blank[:, D + 1:D + 2], -1.0).then_inc(s("blank_ready"), 1)
            nc.gpsimd.memset(mhalf[:], -0.5).then_inc(s("const_ready"), 1)
            pool.wait_ge(s("const_ready"), 1)

            def ln1(b):
                pool.wait_ge(s("ln1_stats"), b + 1)
                link(nc.gpsimd.tensor_scalar(var1[:], mv1[:, :, 1], EPS, None, ALU.add))
                link(nc.gpsimd.tensor_tensor(rstd1[:], var1[:], mhalf[:], ALU.pow))
                for t in range(TPB):
                    nc.gpsimd.tensor_scalar(h2[:, b * TPB + t, 0:D], x_sb[:, b * TPB + t], mv1[:, t, 0:1], rstd1[:, t:t + 1],
                                            ALU.subtract, ALU.mult).then_inc(s("z1_ready"), 1)

            def h_low(b, n):
                k = 2 * b + n
                pool.wait_ge(s("h_hi_ready"), k + 1)
                nc.gpsimd.tensor_tensor(h_lo[:, n * 512:(n + 1) * 512], h_f[:], h_hi[:, n * 512:(n + 1) * 512].bitcast(F32),
                                        ALU.subtract).then_inc(s("h_lo_ready"), 1)

            def ln2(g):
                b = g * GQ // TPB
                pool.wait_ge(s("ln2_stats"), g + 1)
                link(nc.gpsimd.tensor_scalar(var2[:], mv2[:, :, 1], EPS, None, ALU.add))
                link(nc.gpsimd.tensor_tensor(rstd2[:], var2[:], mhalf[:, 0:GQ], ALU.pow))
                rows = h2[:, g * GQ:(g + 1) * GQ, 0:D]
                for t in range(GQ):
                    ins = nc.gpsimd.tensor_scalar(h2[:, g * GQ + t, 0:D], x_sb[:, g * GQ + t], mv2[:, t, 0:1], rstd2[:, t:t + 1],
                                                  ALU.subtract, ALU.mult)
                link(ins)
                if g == 0:
                    pool.wait_ge(s("mod_ready"), 1 + B)
                scale = mod_b[:, b, 1:2].to_broadcast([P, GQ, D])
                shift = mod_b[:, b, 0:1].to_broadcast([P, GQ, D])
                link(nc.gpsimd.tensor_tensor(rows, rows, scale, ALU.mult))
                nc.gpsimd.tensor_tensor(rows, rows, shift, ALU.add).then_inc(s("h2_ready"), 1)

            def scatter(half, a, n):
                if a == 0:
                    pool.wait_ge(s("route_slots"), half + 1)
                    if half == 0:
                        pool.wait_ge(s("slots_blank"), 16)
                for t in range(a, a + n):
                    for k in range(TOPK):
                        nc.gpsimd.indirect_dma_start(
                            out=slots_dram, out_offset=bass.IndirectOffsetOnAxis(ap=slot_i[:, half, k, t:t + 1], axis=0),
                            in_=h2[:, half * HT + t], in_offset=None).then_inc(s(f"scattered_{half}"), 16)

            ln1(0)
            h_low(0, 0)
            h_low(0, 1)
            for i in range(STEPS):
                if i % TPB == 1 and i // TPB + 1 < B:
                    ln1(i // TPB + 1)
                for where in "ab":
                    r = rounds_of(i, where)
                    if r and r[0] == "P" and r[2] < 2:
                        h_low(r[1], r[2])
                    if r and r[0] == "G" and r[2] == 0:
                        ln2(r[1])
                if ROUTE0 <= i < ROUTE0 + HT // 2:
                    scatter(0, 2 * (i - ROUTE0), 2)
            scatter(1, 0, HT)

            def send(p, u):
                t = p * 2 + u
                pool.wait_ge(s("y_ready"), t + 1)
                pool.sem_inc(s("sent"), 1)
                nc.gpsimd.indirect_dma_start(
                    out=y_dram, out_offset=bass.IndirectOffsetOnAxis(ap=dst_i[:, u, 0:1], axis=0),
                    in_=y_sb[:, u], in_offset=None).then_inc(s(f"y_out_{u}"), 16)

            for half in range(HALVES):
                with pool.Fori(0, TILES // 2) as j:
                    for u in range(2):
                        send(j + half * TILES // 2, u)
            pool.wait_ge(s("y_out_0"), 16 * HALVES * TILES // 2)
            pool.wait_ge(s("y_out_1"), 16 * HALVES * TILES // 2)
            for half in range(HALVES):
                for q in range(4):
                    n = half * 4 + q
                    a = half * HT + q * 4
                    if n >= 2:
                        pool.wait_ge(s("combined"), n - 1)
                    pool.dma_start(yy_bufs[:, n % 2], y_pairs[:, a:a + 4]).then_inc(s("y_in"), 16)
                    pool.wait_ge(s("y_in"), 16 * (n + 1))

        @block.scalar
        def _(act):
            act.dma_start(cT[:], c.rearrange("b k -> k b"), allow_slow_non_contiguous=True).then_inc(s("c_loaded"), 16)
            act.dma_start(b_cols[:, 0:1], bq.rearrange("(d o) -> d o", o=1)).then_inc(s("c_loaded"), 16)
            act.dma_start(b_cols[:, 1:2], bk.rearrange("(d o) -> d o", o=1)).then_inc(s("c_loaded"), 16)
            act.dma_start(bv_bc[:], bv.rearrange("(o d) -> o d", o=1).to_broadcast([P, D])).then_inc(s("c_loaded"), 16)
            act.dma_start(wr_sb[:], w_router).then_inc(s("c_loaded"), 16)
            act.wait_ge(s("c_loaded"), 80)
            nc.scalar.activation(c_exp[:], cT[:], ACT.Exp, scale=-1.0).then_inc(s("c_exp_ready"), 1)
            act.wait_ge(s("wT_mm"), 1)
            nc.scalar.activation(wT_hi[:].rearrange("p a b -> p (a b)"), ps_o[:, 0:3 * D], ACT.Copy).then_inc(s("wT_hi_ready"), 1)

            def round_of(r):
                kind, who, n = r
                if kind == "P" and n < 2:
                    act.wait_ge(s("h_full"), 2 * who + n + 1)
                    if who >= 1:
                        act.wait_ge(s("m_filled"), NTH[("P", who - 1, 7)] + 1)
                    nc.scalar.activation(h_hi[:, n * 512:(n + 1) * 512], h_f[:], ACT.Copy).then_inc(s("h_hi_ready"), 1)
                if kind == "P" and 2 <= n < 6:
                    act.wait_ge(s("m_filled"), NTH[r] + 1)
                    t_hi = (q_hi, k_hi)[(n - 2) // 2]
                    col = (n % 2) * 512
                    nc.scalar.activation(t_hi[:, who % 2, col:col + 512], ps_m[:], ACT.Identity,
                                         bias=b_cols[:, (n - 2) // 2:(n - 2) // 2 + 1]).then_inc(s("qk_hi"), 1)
                if kind == "G" and n == 1:
                    act.wait_ge(s("m_filled"), NTH[r] + 1)
                    nc.scalar.activation(h2T[:], ps_m[:], ACT.Copy).then_inc(s("m_freed"), 1)

            for n in range(8):
                round_of(("P", 0, n))
            for i in range(STEPS):
                if i >= 9 and (i - 9) % GQ == 0:
                    g = (i - 9) // GQ
                    act.wait_ge(s("pv_part"), 4 * (g + 1))
                    if g >= 1:
                        act.wait_ge(s("m_filled"), NTH[("G", g - 1, 0)] + 1)
                    nc.scalar.activation(oT[:], ps_o[:], ACT.Copy,
                                         scale=mod_a[:, 2, g * GQ // TPB:g * GQ // TPB + 1]).then_inc(s("o_scaled"), 1)
                if i < NT:
                    act.wait_ge(s("max_ready"), i + 1)
                    if i >= 2:
                        act.wait_ge(s("turned"), 2 * (i - 1))
                    nc.scalar.activation(probs[:, i % 2], ps_s[:, i % 2], ACT.Exp, bias=nmax[:, i:i + 1],
                                         accum_out=rsum[:, i:i + 1]).then_inc(s("exp_ready"), 1)
                if rounds_of(i, "a"):
                    round_of(rounds_of(i, "a"))
                if 1 <= i <= NT:
                    j = i - 1
                    act.wait_ge(s("turned"), 2 * j + 1)
                    if j // GQ >= 2 and j % GQ == 0:
                        act.wait_ge(s("pv_part"), 4 * (j // GQ - 1))
                    q = j % GQ
                    nc.scalar.activation(pT[:, j // GQ % 2, 0:4, q * P:(q + 1) * P], ps_t[:, 0:4], ACT.Copy).then_inc(s("copied_act"), 1)
                if rounds_of(i, "b"):
                    round_of(rounds_of(i, "b"))
                if i in (ROUTE0, STEPS - 1):
                    half = 0 if i == ROUTE0 else 1
                    act.wait_ge(s("route_sub"), half + 1)
                    nc.scalar.activation(r_exp[:], r_sub[:], ACT.Exp).then_inc(s("route_exp"), 1)

            def ffn(p, u, has_gelu, has_copy):
                t = p * 2 + u
                if has_gelu:
                    act.wait_ge(s("hid_biased"), t + 1)
                    if not isinstance(p, int) or t >= 2:
                        act.wait_ge(s("g_turned"), t - 1)
                    nc.scalar.activation(gl[:, 0, u], hb[:, u, 0:HID], ACT.Gelu_apprx_tanh).then_inc(s("gelu_ready"), 1)
                if has_copy:
                    act.wait_ge(s("g_turned"), t)
                    if not isinstance(p, int) or t >= 3:
                        act.wait_ge(s("y_mm"), t - 2)
                    nc.scalar.activation(gl[:, 1, 1 - u], ps_t[:, (1 - u) * 4:(1 - u) * 4 + 4].rearrange("p a b -> p (a b)"), ACT.Copy).then_inc(s("g_copied"), 1)

            for half in range(HALVES):
                p0 = half * TILES // 2
                ffn(p0 + 0, 0, True, False)
                ffn(p0 + 0, 1, True, True)
                with act.Fori(0, (TILES - 2) // 2) as j:
                    for u in range(2):
                        ffn(j + (p0 + 1), u, True, True)
                ffn(p0 + TILES // 2, 0, False, True)

        @block.vector
        def _(dve):
            chain = [0]

            def link(ins):
                chain[0] += 1
                ins.then_inc(s("dve_chain"), 1)
                dve.wait_ge(s("dve_chain"), chain[0])

            def ln1_stats(b, a, z):
                if a == 0:
                    dve.wait_ge(s("x_loaded"), 16 * (b + 1))
                    if b >= 1:
                        dve.wait_ge(s("z1_ready"), TPB * b)
                for t0 in range(a, z, GQ):
                    for t in range(t0, t0 + GQ):
                        ins = nc.vector.bn_stats(stats[:, t - t0], x_sb[:, b * TPB + t])
                    link(ins)
                    for t in range(t0, t0 + GQ):
                        ins = nc.vector.bn_aggr(mv1[:, t], stats[:, t - t0])
                    link(ins)
                if z == TPB:
                    nc.vector.memset(sgn_a[0:1, 0:1], 0.0).then_inc(s("ln1_stats"), 1)

            def clamp(g, sgn):
                link(nc.vector.tensor_scalar(sgn, g, 0.0, 2.0, ALU.is_ge, ALU.mult))
                link(nc.vector.scalar_tensor_tensor(g, g, -1.0, g, ALU.mult, ALU.max))
                link(nc.vector.tensor_scalar(g, g, 0.25, None, ALU.max))
                nc.vector.scalar_tensor_tensor(g, sgn, -1.0, g, ALU.add, ALU.mult).then_inc(s("mod_ready"), 1)

            dve.wait_ge(s("c_exp_ready"), 1)
            link(nc.vector.tensor_scalar(c_exp[:], c_exp[:], 1.0, None, ALU.add))
            link(nc.vector.reciprocal(c_exp[:], c_exp[:]))
            link(nc.vector.tensor_tensor(c_silu[:], c_exp[:], cT[:], ALU.mult))
            dve.wait_ge(s("const_ready"), 1)
            for b in range(B):
                ins = nc.vector.tensor_scalar(c_rep[:, b], ones[:], c_silu[:, b:b + 1], None, ALU.mult)
            ins.then_inc(s("c_silu_ready"), 1)
            ln1_stats(0, 0, TPB)
            dve.wait_ge(s("wT_hi_ready"), 1)
            nc.vector.tensor_tensor(wT_lo[:].rearrange("p a b -> p (a b)"), ps_o[:, 0:3 * D],
                                    wT_hi[:].bitcast(F32).rearrange("p a b -> p (a b)"), ALU.subtract).then_inc(s("wT_lo_ready"), 1)
            dve.wait_ge(s("mod_mm"), 1)
            m = ps_t[:, 0, 0:6 * B].rearrange("p (j b) -> p j b", b=B)
            nc.vector.tensor_copy(mod_a[:, 0], m[:, 0])
            nc.vector.tensor_scalar(mod_a[:, 1], m[:, 1], 1.0, None, ALU.add)
            link(nc.vector.tensor_copy(mod_a[:, 2], m[:, 2]))
            clamp(mod_a[:, 2], sgn_a[:])
            for b in range(B):
                dve.wait_ge(s("mod_mm"), 2 + b)
                m = ps_s[:, b // 2, (b % 2) * 512:(b % 2) * 512 + 3 * D].rearrange("p (j f) -> p j f", j=3)
                nc.vector.tensor_copy(mod_b[:, b, 0], m[:, 0])
                nc.vector.tensor_scalar(mod_b[:, b, 1], m[:, 1], 1.0, None, ALU.add)
                link(nc.vector.tensor_copy(mod_b[:, b, 2], m[:, 2]))
                clamp(mod_b[:, b, 2], sgn_b[:])
                dve.wait_ge(s("mod_ready"), 2 + b)

            def round_of(r):
                kind, who, n = r
                if kind == "P" and n < 2:
                    dve.wait_ge(s("m_filled"), NTH[r] + 1)
                    if 2 * who + n >= 1:
                        dve.wait_ge(s("h_lo_ready"), 2 * who + n)
                    ins = nc.vector.tensor_scalar(h_f[:], ps_m[:], mod_a[:, 1, who:who + 1], mod_a[:, 0, who:who + 1],
                                                  ALU.mult, ALU.add)
                    ins.then_inc(s("h_full"), 1)
                    dve.wait_ge(s("h_full"), 2 * who + n + 1)
                    nc.vector.memset(sgn_a[0:1, 0:1], 0.0).then_inc(s("m_freed"), 1)
                if kind == "P" and 2 <= n < 6:
                    dve.wait_ge(s("qk_hi"), 4 * who + n - 1)
                    w = (n - 2) // 2
                    t_hi, t_lo = ((q_hi, q_lo), (k_hi, k_lo))[w]
                    col = (n % 2) * 512
                    nc.vector.scalar_tensor_tensor(t_lo[:, who % 2, col:col + 512], ps_m[:], b_cols[:, w:w + 1],
                                                   t_hi[:, who % 2, col:col + 512].bitcast(F32),
                                                   ALU.add, ALU.subtract).then_inc(s("m_freed"), 1)
                if kind == "P" and n >= 6:
                    dve.wait_ge(s("m_filled"), NTH[r] + 1)
                    a = (n - 6) * GQ
                    nc.vector.tensor_tensor(v_sb[:, who % 2, a:a + GQ], ps_m[:].rearrange("p (a b) -> p a b", a=GQ),
                                            bv_bc[:].rearrange("p (o d) -> p o d", o=1).to_broadcast([P, GQ, D]),
                                            ALU.add).then_inc(s("m_freed"), 1)
                if kind == "G" and n == 0:
                    a = who * GQ
                    link(nc.vector.reciprocal(rinv[:, a:a + GQ], rsum[:, a:a + GQ]))
                    dve.wait_ge(s("m_filled"), NTH[r] + 1)
                    for t in range(a, a + GQ):
                        ins = nc.vector.scalar_tensor_tensor(x_sb[:, t], ps_m[:, (t - a) * P:(t - a + 1) * P], rinv[:, t:t + 1],
                                                             x_sb[:, t], ALU.mult, ALU.add)
                    ins.then_inc(s("m_freed"), 1)
                    dve.wait_ge(s("m_freed"), NTH[r] + 1)
                    for t in range(a, a + GQ):
                        ins = nc.vector.bn_stats(stats[:, t - a], x_sb[:, t])
                    link(ins)
                    if who >= 1:
                        dve.wait_ge(s("h2_ready"), who)
                    for t in range(a, a + GQ):
                        ins = nc.vector.bn_aggr(mv2[:, t - a], stats[:, t - a])
                    ins.then_inc(s("ln2_stats"), 1)
                    dve.wait_ge(s("ln2_stats"), who + 1)
                if kind == "G" and n == 2:
                    dve.wait_ge(s("m_filled"), NTH[r] + 1)
                    a = who * GQ
                    nc.vector.tensor_copy(logits[:, a:a + GQ], ps_m[:, 0:GQ * E].rearrange("p (t e) -> p t e", e=E)).then_inc(s("m_freed"), 1)
                    dve.wait_ge(s("m_freed"), NTH[r] + 1)

            def bc_t(ap):
                return ap.rearrange("p (t o) -> p t o", o=1).to_broadcast([P, HT, E])

            def route(half):
                a = half * HT
                lg = logits[:, a:a + HT]
                link(nc.vector.tensor_reduce(r_max[:], lg, AX.X, ALU.max))
                nc.vector.tensor_tensor(r_sub[:], lg, bc_t(r_max[:]), ALU.subtract).then_inc(s("route_sub"), 1)
                dve.wait_ge(s("route_exp"), half + 1)
                link(nc.vector.tensor_reduce(r_sum[:], r_exp[:], AX.X, ALU.add))
                link(nc.vector.reciprocal(r_inv[:], r_sum[:]))
                link(nc.vector.tensor_tensor(r_prob[:], r_exp[:], bc_t(r_inv[:]), ALU.mult))
                for t in range(HT):
                    ins = nc.vector.max(top_w[:, a + t], r_prob[:, t])
                link(ins)
                for t in range(HT):
                    ins = nc.vector.max_index(top_i[:, t], top_w[:, a + t], r_prob[:, t])
                link(ins)
                link(nc.vector.tensor_copy(top_f[:], top_i[:, :, 0:TOPK]))
                nc.vector.tensor_copy(h2[:, a:a + HT, D + 1], top_f[:, :, 1])
                for k in range(TOPK):
                    ins = nc.vector.tensor_tensor(hot[:, k], iota_e[:].rearrange("p (o e) -> p o e", o=1).to_broadcast([P, HT, E]),
                                                  top_f[:, :, k:k + 1].to_broadcast([P, HT, E]), ALU.is_equal)
                link(ins)
                nc.vector.tensor_tensor(hot2[:], hot[:, 0], hot[:, 1], ALU.add).then_inc(s("route_hot"), 1)
                dve.wait_ge(s("route_mm"), half + 1)
                n_te = HT * E
                link(nc.vector.tensor_copy(totals[:], ps_m[:, n_te:2 * n_te].rearrange("p (t e) -> p e t", e=E)))
                link(nc.vector.tensor_tensor_scan(upto[:].rearrange("p e t -> p (e t)"), keep[:].rearrange("p e t -> p (e t)"),
                                                  totals[:].rearrange("p e t -> p (e t)"), 0.0, ALU.mult, ALU.add))
                link(nc.vector.tensor_tensor(cmp_n[:], upto[:, :, HT - 1:HT].to_broadcast([P, E, THR]),
                                        thr[:].rearrange("p (o j) -> p o j", o=1).to_broadcast([P, E, THR]), ALU.is_gt))
                link(nc.vector.tensor_tensor(upto[:], upto[:], totals[:], ALU.subtract))
                link(nc.vector.tensor_reduce(n_tiles[:], cmp_n[:], AX.X, ALU.add))
                link(nc.vector.tensor_tensor_scan(end_t[:], ones[:, 0:E], n_tiles[:], 0.0, ALU.mult, ALU.add))
                link(nc.vector.tensor_tensor(base_e[:], end_t[:], n_tiles[:], ALU.subtract))
                link(nc.vector.tensor_scalar(base_e[:], base_e[:], float(P), float(half * TILES * P), ALU.mult, ALU.add))
                link(nc.vector.tensor_tensor(pos[:], ps_m[:, 0:n_te].rearrange("p (t e) -> p t e", e=E),
                                             upto[:].rearrange("p e t -> p t e"), ALU.add))
                link(nc.vector.tensor_tensor(pos[:], pos[:], base_e[:].rearrange("p (o e) -> p o e", o=1).to_broadcast([P, HT, E]), ALU.add))
                for k in range(TOPK):
                    ins = nc.vector.tensor_tensor(pos_k[:, k], pos[:], hot[:, k], ALU.mult)
                link(ins)
                link(nc.vector.tensor_reduce(slot_f[:], pos_k[:], AX.X, ALU.add))
                nc.vector.tensor_copy(slot_i[:, half], slot_f[:]).then_inc(s("route_slots"), 1)
                link(nc.vector.tensor_tensor(cmp_t, iota_t[:].rearrange("p (t o) -> p t o", o=1).to_broadcast([P, TILES, E]),
                                             end_t[:].rearrange("p (o e) -> p o e", o=1).to_broadcast([P, TILES, E]), ALU.is_ge))
                te = tile_e[:, half * TILES:(half + 1) * TILES]
                link(nc.vector.tensor_reduce(te, cmp_t, AX.X, ALU.add))
                link(nc.vector.tensor_scalar(te, te, float(E - 1), None, ALU.min))
                nc.vector.tensor_copy(tile_i[:, half * TILES:(half + 1) * TILES], te).then_inc(s("route_tiles"), 1)
                dve.wait_ge(s("route_tiles"), half + 1)

            for n in range(8):
                round_of(("P", 0, n))
            for i in range(STEPS):
                if i < NT:
                    dve.wait_ge(s("scores"), i + 1)
                    nc.vector.tensor_reduce(nmax[:, i:i + 1], ps_s[:, i % 2], AX.X, ALU.max, negate=True).then_inc(s("max_ready"), 1)
                if i % TPB < 2 and i // TPB + 1 < B:
                    ln1_stats(i // TPB + 1, GQ * (i % TPB), GQ * (i % TPB) + GQ)
                if rounds_of(i, "a"):
                    round_of(rounds_of(i, "a"))
                if 1 <= i <= NT:
                    j = i - 1
                    dve.wait_ge(s("turned"), 2 * j + 2)
                    if j // GQ >= 2 and j % GQ == 0:
                        dve.wait_ge(s("pv_part"), 4 * (j // GQ - 1))
                    q = j % GQ
                    nc.vector.tensor_copy(pT[:, j // GQ % 2, 4:8, q * P:(q + 1) * P], ps_t[:, 4:8]).then_inc(s("copied_dve"), 1)
                if rounds_of(i, "b"):
                    round_of(rounds_of(i, "b"))
                if 2 <= i < 2 + E:
                    e = i - 2
                    dve.wait_ge(s("w1_loaded"), 16 * (e + 1))
                    link(nc.vector.tensor_copy(w1_hl[:, e, 0], w1_raw[:, e % 2]))
                    nc.vector.tensor_tensor(w1_hl[:, e, 1], w1_raw[:, e % 2], w1_hl[:, e, 0].bitcast(F32),
                                            ALU.subtract).then_inc(s("w1_split"), 1)
                if i == ROUTE0:
                    route(0)
            route(1)
            dve.wait_ge(s("bias_loaded"), 32)

            def ffn(p, u, has_x, has_bias, has_y):
                late = not isinstance(p, int)
                t = p * 2 + u
                if has_x:
                    dve.wait_ge(s("xT_mm"), t + 2)
                    if late or t >= 1:
                        dve.wait_ge(s("hid_mm"), t)
                    src = ps_m[:, 0:P] if u == 0 else ps_o[:, 0:P]
                    nc.vector.tensor_copy(xT_hi[:, 1 - u], src).then_inc(s("xT_hi_ready"), 1)
                    dve.wait_ge(s("xT_hi_ready"), t + 2)
                    nc.vector.tensor_tensor(xT_lo[:, 1 - u], src, xT_hi[:, 1 - u].bitcast(F32), ALU.subtract).then_inc(s("xT_ready"), 1)
                    nc.vector.tensor_scalar(dst_f[:, bass.ds(t + 1, 1)], xs[:, 1 - u, D + 1:D + 2], tile_e[:, bass.ds(t + 1, 1)],
                                            xs[:, 1 - u, D:D + 1], ALU.is_equal, ALU.add).then_inc(s("dst_ready"), 1)
                if has_bias:
                    dve.wait_ge(s("hid_mm"), t + 1)
                    if late or t >= 2:
                        dve.wait_ge(s("gelu_ready"), t - 1)
                    nc.vector.tensor_tensor(hb[:, u, 0:HID], ps_s[:, u, 0:HID], b1_bc[:, bass.ds(e_of(t) * HID, HID)],
                                            ALU.add).then_inc(s("hid_biased"), 1)
                if has_y:
                    dve.wait_ge(s("y_mm"), t - 1)
                    if late or t >= 4:
                        q, v = earlier(p, u, 4)
                        dve.wait_ge(s(f"y_out_{v}"), (q + 1) * 16)
                    nc.vector.tensor_tensor(y_sb[:, u], ps_s[:, u, 512:512 + D], b2_bc[:, bass.ds(e_of(t - 2) * D, D)],
                                            ALU.add)
                    dve.wait_ge(s("dst_ready"), t - 1)
                    nc.vector.tensor_tensor(dst_i[:, u], dst_f[:, bass.ds(t - 2, 1)], trash[:, bass.ds(t - 2, 1)], ALU.min).then_inc(s("y_ready"), 1)

            def e_of(t):
                return dve.value_load(tile_i[0:1, bass.ds(t, 1)], min_val=0, max_val=E - 1)

            for half in range(HALVES):
                p0 = half * TILES // 2
                ffn(p0 + -1, 1, True, False, False)
                ffn(p0 + 0, 0, True, True, False)
                ffn(p0 + 0, 1, True, True, False)
                ffn(p0 + 1, 0, True, True, True)
                ffn(p0 + 1, 1, True, True, True)
                with dve.Fori(0, (TILES - 6) // 2) as j:
                    for u in range(2):
                        ffn(j + (p0 + 2), u, True, True, True)
                ffn(p0 + TILES // 2 - 1, 0, True, True, True)
                ffn(p0 + TILES // 2 - 1, 1, False, True, True)
                ffn(p0 + TILES // 2, 0, False, False, True)
                ffn(p0 + TILES // 2, 1, False, False, True)

            for n in range(4 * HALVES):
                a = n * 4
                b = a // TPB
                dve.wait_ge(s("y_in"), 16 * (n + 1))
                yy = yy_bufs[:, n % 2]
                for t in range(4):
                    ins = nc.vector.tensor_scalar(yy[:, t, 0:D], yy[:, t, 0:D], top_w[:, a + t, 0:1], None, ALU.mult)
                link(ins)
                for t in range(4):
                    ins = nc.vector.scalar_tensor_tensor(yy[:, t, 0:D], yy[:, t, D:2 * D], top_w[:, a + t, 1:2], yy[:, t, 0:D], ALU.mult, ALU.add)
                link(ins)
                link(nc.vector.tensor_tensor(yy[:, :, 0:D], yy[:, :, 0:D], mod_b[:, b, 2:3].to_broadcast([P, 4, D]), ALU.mult))
                nc.vector.tensor_tensor(x_sb[:, a:a + 4], x_sb[:, a:a + 4], yy[:, :, 0:D], ALU.add).then_inc(s("combined"), 1)

        @block.tensor
        def _(pe):
            def product3(o, l_hi, l_lo, r_hi, r_lo, first=True, last=True):
                nc.tensor.matmul(o, l_hi, r_hi, start=first, stop=False)
                nc.tensor.matmul(o, l_hi, r_lo, start=False, stop=False)
                return nc.tensor.matmul(o, l_lo, r_hi, start=False, stop=last)

            pe.wait_ge(s("w_loaded"), 48)
            pe.wait_ge(s("ident_ready"), 1)
            for w in range(3):
                ins = nc.tensor.transpose(ps_o[:, w * D:(w + 1) * D], w_raw[:, w], ident[:])
            ins.then_inc(s("wT_mm"), 1)
            pe.wait_ge(s("wmod_loaded"), 16)
            pe.wait_ge(s("c_silu_ready"), 1)
            for j in range(6):
                ins = nc.tensor.matmul(ps_t[:, 0, j * B:(j + 1) * B], wmod_sb[:, j], c_silu[:], start=True, stop=True)
            ins.then_inc(s("mod_mm"), 1)
            for b in range(B):
                nc.tensor.matmul(ps_s[:, b // 2, (b % 2) * 512:(b % 2) * 512 + 3 * D], c_rep[:, b],
                                 wmod_sb[:, 3:6].rearrange("p a b -> p (a b)"), start=True, stop=True).then_inc(s("mod_mm"), 1)

            def round_of(r):
                kind, who, n = r
                if NTH[r] >= 1:
                    pe.wait_ge(s("m_freed"), NTH[r])
                if kind == "P" and n < 2:
                    pe.wait_ge(s("z1_ready"), who * TPB + (n + 1) * GQ)
                    for t in range(GQ):
                        ins = nc.tensor.transpose(ps_m[:, t * P:(t + 1) * P], h2[:, who * TPB + n * GQ + t, 0:D], ident[:])
                if kind == "P" and 2 <= n < 6:
                    if n == 2:
                        pe.wait_ge(s("h_lo_ready"), 2 * who + 2)
                        if who == 0:
                            pe.wait_ge(s("wT_lo_ready"), 1)
                    w, col = (n - 2) // 2, (n % 2) * 512
                    ins = product3(ps_m[:], wT_hi[:, w], wT_lo[:, w], h_hi[:, col:col + 512], h_lo[:, col:col + 512])
                if kind == "P" and n >= 6:
                    for t in range(GQ):
                        a = ((n - 6) * GQ + t) * P
                        ins = product3(ps_m[:, t * P:(t + 1) * P], h_hi[:, a:a + P], h_lo[:, a:a + P], wT_hi[:, 2], wT_lo[:, 2])
                if kind == "G" and n == 0:
                    pe.wait_ge(s("o_scaled"), who + 1)
                    for t in range(GQ):
                        ins = nc.tensor.transpose(ps_m[:, t * P:(t + 1) * P], oT[:, t * P:(t + 1) * P], ident[:])
                if kind == "G" and n == 1:
                    pe.wait_ge(s("h2_ready"), who + 1)
                    for t in range(GQ):
                        ins = nc.tensor.transpose(ps_m[:, t * P:(t + 1) * P], h2[:, who * GQ + t, 0:D], ident[:])
                if kind == "G" and n == 2:
                    for t in range(GQ):
                        ins = nc.tensor.matmul(ps_m[:, t * E:(t + 1) * E], h2T[:, t * P:(t + 1) * P], wr_sb[:], start=True, stop=True)
                ins.then_inc(s("m_filled"), 1)

            def route_counts(half):
                pe.wait_ge(s("route_hot"), half + 1)
                m = hot2[:].rearrange("p t e -> p (t e)")
                nc.tensor.matmul(ps_m[:, 0:HT * E], before[:], m, start=True, stop=True)
                nc.tensor.matmul(ps_m[:, HT * E:2 * HT * E], ones[:], m, start=True, stop=True).then_inc(s("route_mm"), 1)

            for n in range(8):
                round_of(("P", 0, n))
            pe.wait_ge(s("mod_ready"), 1 + B)
            for i in range(STEPS):
                if i < NT:
                    b = i // TPB
                    if i >= 2:
                        pe.wait_ge(s("exp_ready"), i - 1)
                    if i % TPB == 0:
                        pe.wait_ge(s("m_freed"), NTH[("P", b, 5)] + 1)
                    q = (i % TPB) * P
                    for half in range(2):
                        ins = product3(ps_s[:, i % 2, half * 512:(half + 1) * 512], q_hi[:, b % 2, q:q + P], q_lo[:, b % 2, q:q + P],
                                       k_hi[:, b % 2, half * 512:(half + 1) * 512], k_lo[:, b % 2, half * 512:(half + 1) * 512])
                    ins.then_inc(s("scores"), 1)
                if rounds_of(i, "a"):
                    round_of(rounds_of(i, "a"))
                g, part = (i - 5) // GQ, (i - 5) % GQ
                if 0 <= i - 5 and g < NG:
                    if part == 0:
                        pe.wait_ge(s("copied_act"), GQ * (g + 1))
                        pe.wait_ge(s("copied_dve"), GQ * (g + 1))
                        pe.wait_ge(s("m_freed"), NTH[("P", g * GQ // TPB, 7)] + 1)
                        if g >= 1:
                            pe.wait_ge(s("o_scaled"), g)
                    for kb in (2 * part, 2 * part + 1):
                        ins = nc.tensor.matmul(ps_o[:], v_sb[:, g * GQ // TPB % 2, kb], pT[:, g % 2, kb], start=(kb == 0), stop=(kb == TPB - 1))
                    ins.then_inc(s("pv_part"), 1)
                if 1 <= i <= NT:
                    j = i - 1
                    pe.wait_ge(s("exp_ready"), j + 1)
                    for h in range(2):
                        if j >= 1:
                            pe.wait_ge(s(("copied_act", "copied_dve")[h]), j)
                        for kb in range(4 * h, 4 * h + 4):
                            ins = nc.tensor.transpose(ps_t[:, kb], probs[:, j % 2, kb * P:(kb + 1) * P], ident[:])
                        ins.then_inc(s("turned"), 1)
                if rounds_of(i, "b"):
                    round_of(rounds_of(i, "b"))
                if i == ROUTE0:
                    route_counts(0)
                    pe.wait_ge(s("route_tiles"), 1)
            route_counts(1)
            pe.wait_ge(s("route_tiles"), 2)
            pe.wait_ge(s("w1_split"), E)
            pe.wait_ge(s("w2_loaded"), 16)

            def e_of(t):
                return pe.value_load(tile_i[0:1, bass.ds(t, 1)], min_val=0, max_val=E - 1)

            def ffn(p, u, has_x, has_first, has_turn, has_second):
                late = not isinstance(p, int)
                t = p * 2 + u
                if has_x:
                    q, v = earlier(p, u, -1)
                    pe.wait_ge(s(f"x_in_{v}"), (q + 1) * 16)
                    if late or t >= 1:
                        pe.wait_ge(s("xT_ready"), t)
                    dst = ps_m[:, 0:P] if u == 0 else ps_o[:, 0:P]
                    nc.tensor.transpose(dst, xs[:, 1 - u, 0:D], ident[:]).then_inc(s("xT_mm"), 1)
                if has_first:
                    pe.wait_ge(s("xT_ready"), t + 1)
                    if late or t >= 2:
                        pe.wait_ge(s("hid_biased"), t - 1)
                    w = w1_hl[:].rearrange("p e a h -> p (e a h)")
                    e = e_of(t)
                    product3(ps_s[:, u, 0:HID], xT_hi[:, u], xT_lo[:, u], w[:, bass.ds(e * (2 * HID), HID)],
                             w[:, bass.ds(e * (2 * HID) + HID, HID)]).then_inc(s("hid_mm"), 1)
                if has_turn:
                    pe.wait_ge(s("gelu_ready"), t)
                    if late or t >= 3:
                        pe.wait_ge(s("g_copied"), t - 2)
                    for j in range(HB):
                        ins = nc.tensor.transpose(ps_t[:, (1 - u) * 4 + j], gl[:, 0, 1 - u, j * P:(j + 1) * P], ident[:])
                    ins.then_inc(s("g_turned"), 1)
                if has_second:
                    pe.wait_ge(s("g_copied"), t - 1)
                    if late or t >= 4:
                        pe.wait_ge(s("y_ready"), t - 3)
                    w = w2_sb[:].rearrange("p e j d -> p (e j d)")
                    e = e_of(t - 2)
                    for j in range(HB):
                        ins = nc.tensor.matmul(ps_s[:, u, 512:512 + D], gl[:, 1, u, j * P:(j + 1) * P],
                                               w[:, bass.ds(e * (HB * D) + j * D, D)], start=(j == 0), stop=(j == HB - 1))
                    ins.then_inc(s("y_mm"), 1)

            for half in range(HALVES):
                p0 = half * TILES // 2
                ffn(p0 + -1, 1, True, False, False, False)
                ffn(p0 + 0, 0, True, True, False, False)
                ffn(p0 + 0, 1, True, True, True, False)
                ffn(p0 + 1, 0, True, True, True, True)
                ffn(p0 + 1, 1, True, True, True, True)
                with pe.Fori(0, (TILES - 6) // 2) as j:
                    for u in range(2):
                        ffn(j + (p0 + 2), u, True, True, True, True)
                ffn(p0 + TILES // 2 - 1, 0, True, True, True, True)
                ffn(p0 + TILES // 2 - 1, 1, False, True, True, True)
                ffn(p0 + TILES // 2, 0, False, False, True, True)
                ffn(p0 + TILES // 2, 1, False, False, False, True)


_INS = ['L0_attn_x', 'L0_attn_Wq', 'L0_attn_bq', 'L0_attn_Wk', 'L0_attn_bk', 'L0_attn_Wv', 'L0_attn_bv',
        'L0_ffn_w_router', 'L0_ffn_w1', 'L0_ffn_b1', 'L0_ffn_w2', 'L0_ffn_b2', 'L0_c', 'L0_wmod']


def kernel(**inputs):
    import numpy as _np
    import concourse.bacc as _bacc
    from concourse import mybir as _mybir
    from concourse.bass_utils import run_bass_kernel_spmd as _run

    nc = _bacc.Bacc("TRN2", target_bir_lowering=False, num_devices=1)
    arrays, args = {}, []
    for name in _INS:
        a = _np.ascontiguousarray(inputs[name])
        arrays[f"in_{name}_dram"] = a
        args.append(nc.dram_tensor(f"in_{name}_dram", a.shape, _mybir.dt.from_np(a.dtype), kind="ExternalInput").ap())
    args.append(nc.dram_tensor("out_dram", (B, SEQ, D), F32, kind="ExternalOutput").ap())
    build(nc, *args)
    r = _run(nc, [arrays], core_ids=[0])
    return r.results[0]["out_dram"]
```

```python
from contextlib import ExitStack

import concourse.bass as bass
from concourse import mybir

ALU = mybir.AluOpType
ACT = mybir.ActivationFunctionType
AX = mybir.AxisListType
F32 = mybir.dt.float32
F32R = mybir.dt.float32r
I32 = mybir.dt.int32
U32 = mybir.dt.uint32

P = 128
D = 128
B = 4
SEQ = 1024
TPB = SEQ // P
NT = B * TPB
GQ = 4
NG = NT // GQ
E = 8
HID = 512
HB = HID // P
TOPK = 2
HALVES = 2
HT = NT // HALVES
TILES = (HT * P * TOPK + E * (P - 1)) // P
TILES += TILES % 2
ROW = D + 2
PAIRS = NT * P * TOPK
NSLOT = HALVES * TILES * P
EPS = 1e-5
THR = HT

ROUNDS_A = {2: ("P", 0), 3: ("P", 2), 4: ("P", 3), 5: ("P", 4), 6: ("P", 5), 7: ("P", 7)}
ROUNDS_B = {0: ("G", 2), 1: ("G", 0), 2: ("P", 1), 3: ("G", 1), 4: ("G", 2), 5: ("G", 0), 6: ("P", 6), 7: ("G", 1)}
MODS = {(0, "a"): 0, (0, "b"): 1, (1, "a"): 2, (1, "b"): 3}
TAIL = {NT + 1: (None, ("G", NG - 2, 0)), NT + 2: (None, ("G", NG - 1, 0)),
        NT + 3: (("G", NG - 2, 1), ("G", NG - 2, 2)), NT + 4: (("G", NG - 1, 1), ("G", NG - 1, 2))}
STEPS = NT + 5
ROUTE0 = HT + 8
NBUF = 4
ALL_TILES = HALVES * TILES
CHUNK = 4
NCHUNK = NT // CHUNK
W1_STEPS = [2, 3, 6, 8, 10, 11, 14, 16]


def rounds_of(i, where):
    if i > NT:
        return TAIL[i]["ab".index(where)]
    if where == "a" and i == ROUTE0 + 2:
        return ("R", 0, 0)
    if (i, where) in MODS:
        return ("M", MODS[i, where], 0)
    r = (ROUNDS_A if where == "a" else ROUNDS_B).get(i % TPB)
    if r is None:
        return None
    kind, n = r
    if kind == "P":
        b = i // TPB + 1
        return ("P", b, n) if b < B else None
    last = {0: 9, 1: 11, 2: 12}[n]
    if (i - last) % GQ or i < last:
        return None
    return ("G", (i - last) // GQ, n)


def parts_of(i):
    if i == NT + 1:
        return [(NG - 1, n) for n in range(4)]
    return [((i - 5) // GQ, (i - 5) % GQ)] if 5 <= i <= NT else []


def all_rounds():
    order = [("P", 0, n) for n in range(8)]
    for i in range(STEPS):
        order += [r for r in (rounds_of(i, "a"), rounds_of(i, "b")) if r]
    return order + [("R", 1, 0)]


def schedule():
    order = [("attend", i) for i in range(NT + 3)]
    order += [("tile", -1), ("tile", 0), ("attend", NT + 3), ("tile", 1), ("tile", 2), ("attend", NT + 4)]
    for t in range(3, ALL_TILES + 2):
        order.append(("tile", t))
        if t % 2 and 5 <= t < 5 + 2 * ROUTE_STAGES:
            order.append(("route", (t - 5) // 2))
        n, rest = divmod(t - TILES - 8, 6)
        if rest == 0 and 0 <= n < NCHUNK // HALVES:
            order.append(("chunk", n))
    return order + [("chunk", n) for n in range(NCHUNK // HALVES, NCHUNK)]


ROUTE_STAGES = 7


def build(nc, x, Wq, bq, Wk, bk, Wv, bv, w_router, w1, b1, w2, b2, c, wmod, out):
    NTH = {r: n for n, r in enumerate(all_rounds())}
    ORDER = schedule()

    with ExitStack() as ctx:
        def sb(name, shape, dt=F32):
            return ctx.enter_context(nc.sbuf_tensor(name, shape, dt))

        def sem(name):
            return ctx.enter_context(nc.semaphore(name))

        ps_s = ctx.enter_context(nc.psum_tensor("ps_s", [P, 2, SEQ], F32))
        ps_t = ctx.enter_context(nc.psum_tensor("ps_t", [P, TPB, P], F32))
        ps_o = ctx.enter_context(nc.psum_tensor("ps_o", [P, GQ * P], F32))
        ps_m = ctx.enter_context(nc.psum_tensor("ps_m", [P, GQ * P], F32))

        ident = sb("ident", [P, P])
        before = sb("before", [P, P])
        ones = sb("ones", [P, P])
        iota_e = sb("iota_e", [P, E])
        iota_t = sb("iota_t", [P, TILES])
        thr = sb("thr", [P, THR])
        keep = sb("keep", [P, E, HT])
        trash = sb("trash", [P, HALVES * TILES])
        mhalf = sb("mhalf", [P, GQ])

        x_sb = sb("x_sb", [P, NT, D])
        wT_hi = sb("wT_hi", [P, 3, D], F32R)
        wT_lo = sb("wT_lo", [P, 3, D], F32R)
        b_cols = sb("b_cols", [P, 2])
        bv_bc = sb("bv_bc", [P, D])
        cT = sb("cT", [P, B])
        c_exp = sb("c_exp", [P, B])
        c_silu = sb("c_silu", [P, B])
        mod_a = sb("mod_a", [P, 3, B])
        sgn_a = sb("sgn_a", [P, B])
        mod_b = sb("mod_b", [P, B, 3, D])
        sgn_b = sb("sgn_b", [P, D])
        wr_sb = sb("wr_sb", [P, E])

        stats = sb("stats", [P, GQ, 6])
        mv1 = sb("mv1", [P, TPB, 2])
        mv2 = sb("mv2", [P, GQ, 2])
        var1 = sb("var1", [P, TPB])
        rstd1 = sb("rstd1", [P, TPB])
        var2 = sb("var2", [P, GQ])
        rstd2 = sb("rstd2", [P, GQ])
        h_f = sb("h_f", [P, GQ * P])
        h_hi = sb("h_hi", [P, SEQ], F32R)
        h_lo = sb("h_lo", [P, SEQ], F32R)
        q_hi = sb("q_hi", [P, 2, SEQ], F32R)
        q_lo = sb("q_lo", [P, 2, SEQ], F32R)
        k_hi = sb("k_hi", [P, 2, SEQ], F32R)
        k_lo = sb("k_lo", [P, 2, SEQ], F32R)
        v_sb = sb("v_sb", [P, 2, TPB, D])
        nmax = sb("nmax", [P, NT])
        rsum = sb("rsum", [P, NT])
        rinv = sb("rinv", [P, NT])
        probs = sb("probs", [P, 2, SEQ])
        pT = sb("pT", [P, 2, TPB, GQ * P])
        early = pT[:, 1].rearrange("p a b -> p (a b)")
        w_raw = early[:, 0:3 * D].rearrange("p (w d) -> p w d", w=3)
        wmod_sb = early[:, 3 * D:9 * D].rearrange("p (j f) -> p j f", j=6)
        c_rep = early[:, 9 * D:(9 + B) * D].rearrange("p (b f) -> p b f", b=B)
        oT = sb("oT", [P, GQ * P])
        h2 = sb("h2", [P, NT, ROW])
        h2T = h_f
        logits = sb("logits", [P, NT, E])

        r_max = sb("r_max", [P, HT])
        r_sub = sb("r_sub", [P, HT, E])
        r_exp = sb("r_exp", [P, HT, E])
        r_sum = sb("r_sum", [P, HT])
        r_inv = sb("r_inv", [P, HT])
        r_prob = sb("r_prob", [P, HT, E])
        top_w = sb("top_w", [P, NT, 8])
        top_i = sb("top_i", [P, HT, 8], U32)
        top_f = sb("top_f", [P, HT, TOPK])
        hot = sb("hot", [P, TOPK, HT, E])
        hot2 = sb("hot2", [P, HT, E])
        totals = sb("totals", [P, E, HT])
        upto = sb("upto", [P, E, HT])
        cmp_n = sb("cmp_n", [P, E, THR])
        n_tiles = sb("n_tiles", [P, E])
        end_t = sb("end_t", [P, E])
        base_e = sb("base_e", [P, E])
        pos = sb("pos", [P, HT, E])
        pos_k = sb("pos_k", [P, TOPK, HT, E])
        slot_f = sb("slot_f", [P, TOPK, HT])
        slot_i = sb("slot_i", [P, HALVES, TOPK, HT], I32)
        cmp_t = sb("cmp_t", [P, TILES, E])
        tile_e = sb("tile_e", [P, HALVES * TILES])
        tile_i = sb("tile_i", [P, HALVES * TILES], I32)

        w1_hl = sb("w1_hl", [P, E, 2, HID], F32R)
        w2_sb = sb("w2_sb", [P, E, HB, D])
        w1_raw = sb("w1_raw", [P, 2, HID])
        blank = sb("blank", [P, ROW])
        xs = sb("xs", [P, NBUF, ROW])
        xT_hi = sb("xT_hi", [P, 2, P], F32R)
        xT_lo = sb("xT_lo", [P, 2, P], F32R)
        hb = probs[:, :, 0:HID]
        gT = probs[:, :, HID:2 * HID]
        gl = v_sb[:, 0].rearrange("p (u a) d -> p u (a d)", u=2)
        b1_bc = pT[:, 0].rearrange("p a b -> p (a b)")
        b2_bc = w1_raw[:].rearrange("p a b -> p (a b)")
        yy = pT[:, 1].rearrange("p a b -> p (a b)").rearrange("p (n t kd) -> p n t kd", n=4, t=CHUNK)
        y_sb = sb("y_sb", [P, NBUF, D])
        dst_f = sb("dst_f", [P, HALVES * TILES])
        dst_i = sb("dst_i", [P, NBUF, 1], I32)
        slots_dram = nc.dram_tensor("slots", (NSLOT, ROW), F32, kind="Internal").ap()
        y_dram = nc.dram_tensor("pairs", (PAIRS + NSLOT, D), F32, kind="Internal").ap()

        S = {n: sem(n) for n in (
            "const_ready ident_ready w_loaded x_loaded c_loaded wmod_loaded w1_loaded w2_loaded w1_split bias_loaded "
            "mod_mm mod_ready c_exp_ready c_silu_ready wT_mm wT_hi_ready wT_lo_ready "
            "ln1_stats rstd1_ready rstd2_ready z1_ready dve_chain pool_chain act_chain "
            "m_filled m_freed h_hi_ready h_lo_ready qk_hi qk_lo v_ready "
            "scores max_ready exp_ready turned copied_act copied_dve pv_part o_scaled x1_ready ln2_stats h2_ready "
            "h2T_ready logits_ready route_sub route_exp route_hot route_slots route_tiles blank_ready "
            "slots_blank scattered_0 scattered_1 x_in_0 x_in_1 x_in_2 x_in_3 xT_mm xT_hi_ready xT_ready hid_mm hid_biased gelu_ready g_turned g_copied "
            "y_mm y_ready dst_ready y_out_0 y_out_1 y_out_2 y_out_3 y_in_0 y_in_1 y_in_2 y_in_3 combined out_done").split()}

        def s(name):
            return S[name]

        x_t = x.rearrange("b (t p) d -> p (b t) d", p=P)
        out_t = out.rearrange("b (t p) d -> p (b t) d", p=P)
        y_pairs = y_dram[0:PAIRS].rearrange("(t p k) d -> p t (k d)", p=P, k=TOPK)
        ps_y = ps_s[:, 0, 512:512 + D]
        ps_x = ps_s[:, 1, 512:512 + D]

        def bank_of(r):
            kind, who, n = r
            if kind != "P" or who or n == 0:
                return ps_m[:]
            if n <= 4:
                return ps_s[:, (n - 1) // 2, (n - 1) % 2 * 512:(n - 1) % 2 * 512 + 512]
            return {5: ps_t[:, 4:8].rearrange("p a b -> p (a b)"), 6: ps_o[:],
                    7: ps_t[:, 0:4].rearrange("p a b -> p (a b)")}[n]

        def load_expert(eng, t):
            return eng.value_load(tile_i[0:1, t:t + 1], min_val=0, max_val=E - 1)

        block = ctx.enter_context(nc.Block())

        @block.sync
        def _(sp):
            for b in range(B):
                sp.dma_start(x_sb[:, b * TPB:(b + 1) * TPB], x_t[:, b * TPB:(b + 1) * TPB]).then_inc(s("x_loaded"), 16)
                if b == 0:
                    for h, w in enumerate((Wq, Wk, Wv)):
                        sp.dma_start(w_raw[:, h], w).then_inc(s("w_loaded"), 16)
                    sp.dma_start(wmod_sb, wmod.rearrange("k (j f) -> k j f", j=6)).then_inc(s("wmod_loaded"), 16)
                sp.wait_ge(s("x_loaded"), 16 * (b + 1))
            sp.dma_start(w2_sb[:], w2.rearrange("e (j p) d -> p e j d", p=P)).then_inc(s("w2_loaded"), 16)
            sp.wait_ge(s("blank_ready"), 1)
            sp.dma_start(slots_dram.rearrange("(p t) r -> p t r", p=P),
                         blank[:].rearrange("p (o r) -> p o r", o=1).to_broadcast([P, ALL_TILES, ROW])).then_inc(s("slots_blank"), 16)
            for e in range(E):
                if e >= 2:
                    sp.wait_ge(s("w1_split"), e - 1)
                if e >= 1:
                    sp.wait_ge(s("w1_loaded"), 16 * e)
                sp.dma_start(w1_raw[:, e % 2], w1[e]).then_inc(s("w1_loaded"), 16)
            sp.wait_ge(s("w1_split"), E)
            sp.dma_start(b2_bc, b2.rearrange("(o e) d -> o (e d)", o=1).to_broadcast([P, E * D])).then_inc(s("bias_loaded"), 16)
            sp.wait_ge(s("pv_part"), 4 * (NG - 1))
            sp.dma_start(b1_bc, b1.rearrange("(o e) h -> o (e h)", o=1).to_broadcast([P, E * HID])).then_inc(s("bias_loaded"), 16)

            def load_tile(t):
                if t % TILES == 0:
                    sp.wait_ge(s(f"scattered_{t // TILES}"), 16 * TOPK * HT)
                if t >= NBUF:
                    sp.wait_ge(s("xT_mm"), t - NBUF + 1)
                    sp.wait_ge(s("dst_ready"), t - NBUF + 1)
                sp.dma_start(xs[:, t % NBUF], slots_dram[t * P:(t + 1) * P]).then_inc(s(f"x_in_{t % NBUF}"), 16)

            def load_pairs(half):
                n_out = (half + 1) * TILES // NBUF
                for u in range(NBUF):
                    sp.wait_ge(s(f"y_out_{u}"), 16 * n_out)
                for n in range(4):
                    if half:
                        sp.wait_ge(s("combined"), n + 1)
                    else:
                        sp.wait_ge(s("pv_part"), NT)
                    a = half * HT + n * CHUNK
                    sp.dma_start(yy[:, n], y_pairs[:, a:a + CHUNK]).then_inc(s(f"y_in_{n}"), 16)

            def store(n):
                sp.wait_ge(s("combined"), n + 1)
                sp.dma_start(out_t[:, n * CHUNK:(n + 1) * CHUNK], x_sb[:, n * CHUNK:(n + 1) * CHUNK]).then_inc(s("out_done"), 16)

            for t in range(NBUF - 1):
                load_tile(t)
            for what, n in ORDER:
                if what == "tile" and 0 <= n < ALL_TILES - NBUF + 1:
                    load_tile(n + NBUF - 1)
                if what == "tile" and n == TILES + 4:
                    load_pairs(0)
                if what == "tile" and n > TILES + 10 and (n - TILES - 10) % 6 == 0 and (n - TILES - 10) // 6 <= 4:
                    store((n - TILES - 10) // 6 - 1)
            load_pairs(1)
            for n in range(4, NCHUNK):
                store(n)
            sp.wait_ge(s("out_done"), 16 * NCHUNK)

        @block.gpsimd
        def _(pool):
            chain = [0]

            def link(ins):
                chain[0] += 1
                ins.then_inc(s("pool_chain"), 1)
                pool.wait_ge(s("pool_chain"), chain[0])

            nc.gpsimd.memset(ident[:], 0.0).then_inc(s("pool_chain"), 1)
            nc.gpsimd.memset(before[:], 0.0).then_inc(s("pool_chain"), 1)
            nc.gpsimd.memset(ones[:], 1.0).then_inc(s("pool_chain"), 1)
            nc.gpsimd.memset(keep[:], 1.0).then_inc(s("pool_chain"), 1)
            chain[0] = 4
            pool.wait_ge(s("pool_chain"), 4)
            nc.gpsimd.affine_select(out=ident[:], in_=ident[:], compare_op=ALU.not_equal, fill=1.0, base=0,
                                    pattern=[[-1, P]], channel_multiplier=1).then_inc(s("ident_ready"), 1)
            nc.gpsimd.affine_select(out=before[:], in_=before[:], compare_op=ALU.is_ge, fill=1.0, base=0,
                                    pattern=[[-1, P]], channel_multiplier=1)
            nc.gpsimd.memset(keep[:, :, 0:1], 0.0)
            f = dict(allow_small_or_imprecise_dtypes=True)
            nc.gpsimd.iota(iota_e[:], [[1, E]], base=0, channel_multiplier=0, **f)
            nc.gpsimd.iota(iota_t[:], [[1, TILES]], base=0, channel_multiplier=0, **f)
            nc.gpsimd.iota(thr[:], [[P, THR]], base=0, channel_multiplier=0, **f)
            nc.gpsimd.iota(trash[:], [[P, HALVES * TILES]], base=PAIRS, channel_multiplier=1, **f)
            nc.gpsimd.iota(h2[:, :, D:D + 1], [[TOPK * P, NT], [1, 1]], base=0, channel_multiplier=TOPK, **f)
            link(nc.gpsimd.memset(blank[:], 0.0))
            link(nc.gpsimd.memset(blank[:, D:D + 1], 1e6))
            nc.gpsimd.memset(blank[:, D + 1:D + 2], -1.0).then_inc(s("blank_ready"), 1)
            nc.gpsimd.memset(mhalf[:], -0.5).then_inc(s("const_ready"), 1)
            pool.wait_ge(s("const_ready"), 1)

            def ln1(b, n):
                pool.wait_ge(s("ln1_stats"), 2 * b + n + 1)
                a = n * GQ
                link(nc.gpsimd.tensor_scalar(var1[:, a:a + GQ], mv1[:, a:a + GQ, 1], EPS, None, ALU.add))
                nc.gpsimd.tensor_tensor(rstd1[:, a:a + GQ], var1[:, a:a + GQ], mhalf[:], ALU.pow).then_inc(s("rstd1_ready"), 1)

            def h_low(b, n):
                k = 2 * b + n
                pool.wait_ge(s("h_hi_ready"), k + 1)
                nc.gpsimd.tensor_tensor(h_lo[:, n * 512:(n + 1) * 512], h_f[:], h_hi[:, n * 512:(n + 1) * 512].bitcast(F32),
                                        ALU.subtract).then_inc(s("h_lo_ready"), 1)

            def ln2(g):
                pool.wait_ge(s("ln2_stats"), g + 1)
                link(nc.gpsimd.tensor_scalar(var2[:], mv2[:, :, 1], EPS, None, ALU.add))
                nc.gpsimd.tensor_tensor(rstd2[:], var2[:], mhalf[:], ALU.pow).then_inc(s("rstd2_ready"), 1)

            def scatter(half, a, n):
                if a == 0:
                    pool.wait_ge(s("route_slots"), half + 1)
                    if half == 0:
                        pool.wait_ge(s("slots_blank"), 16)
                for t in range(a, a + n):
                    for k in range(TOPK):
                        nc.gpsimd.indirect_dma_start(
                            out=slots_dram, out_offset=bass.IndirectOffsetOnAxis(ap=slot_i[:, half, k, t:t + 1], axis=0),
                            in_=h2[:, half * HT + t], in_offset=None).then_inc(s(f"scattered_{half}"), 16)

            def attend(i):
                if i % TPB < 2 and i // TPB + 1 < B:
                    ln1(i // TPB + 1, i % TPB)
                for where in "ab":
                    r = rounds_of(i, where)
                    if r and r[0] == "P" and r[2] < 2:
                        h_low(r[1], r[2])
                    if r and r[0] == "G" and r[2] == 0:
                        ln2(r[1])
                if ROUTE0 + 2 <= i < ROUTE0 + 6:
                    scatter(0, 4 * (i - ROUTE0 - 2), 4)

            def send(t):
                u = t % NBUF
                pool.wait_ge(s("y_ready"), t + 1)
                nc.gpsimd.indirect_dma_start(
                    out=y_dram, out_offset=bass.IndirectOffsetOnAxis(ap=dst_i[:, u, 0:1], axis=0),
                    in_=y_sb[:, u], in_offset=None).then_inc(s(f"y_out_{u}"), 16)

            ln1(0, 0)
            ln1(0, 1)
            h_low(0, 0)
            h_low(0, 1)
            route_end = 5 + 2 * (ROUTE_STAGES - 1)
            for what, n in ORDER:
                if what == "attend":
                    attend(n)
                if what == "tile" and n >= 2:
                    send(n - 2)
                    if route_end + 1 <= n < route_end + 1 + HT:
                        scatter(1, n - route_end - 1, 1)

        @block.scalar
        def _(act):
            act.dma_start(cT[:], c.rearrange("b k -> k b"), allow_slow_non_contiguous=True).then_inc(s("c_loaded"), 16)
            act.dma_start(b_cols[:, 0:1], bq.rearrange("(d o) -> d o", o=1)).then_inc(s("c_loaded"), 16)
            act.dma_start(b_cols[:, 1:2], bk.rearrange("(d o) -> d o", o=1)).then_inc(s("c_loaded"), 16)
            act.dma_start(bv_bc[:], bv.rearrange("(o d) -> o d", o=1).to_broadcast([P, D])).then_inc(s("c_loaded"), 16)
            act.dma_start(wr_sb[:], w_router).then_inc(s("c_loaded"), 16)
            act.wait_ge(s("c_loaded"), 80)
            nc.scalar.activation(c_exp[:], cT[:], ACT.Exp, scale=-1.0).then_inc(s("c_exp_ready"), 1)
            act.wait_ge(s("wT_mm"), 1)
            nc.scalar.activation(wT_hi[:].rearrange("p a b -> p (a b)"), ps_o[:, 0:3 * D], ACT.Copy).then_inc(s("wT_hi_ready"), 1)

            def round_of(r):
                kind, who, n = r
                if kind == "P" and n < 2:
                    act.wait_ge(s("m_freed"), NTH[r] + 1)
                    if who >= 1:
                        act.wait_ge(s("m_filled"), NTH[("P", who - 1, 7)] + 1)
                    nc.scalar.activation(h_hi[:, n * 512:(n + 1) * 512], h_f[:], ACT.Copy).then_inc(s("h_hi_ready"), 1)
                if kind == "P" and 2 <= n < 6:
                    act.wait_ge(s("m_filled"), NTH[r] + 1)
                    t_hi = (q_hi, k_hi)[(n - 2) // 2]
                    col = (n % 2) * 512
                    nc.scalar.activation(t_hi[:, who % 2, col:col + 512], bank_of(r), ACT.Identity,
                                         bias=b_cols[:, (n - 2) // 2:(n - 2) // 2 + 1]).then_inc(s("qk_hi"), 1)
                if kind == "G" and n == 1:
                    act.wait_ge(s("m_filled"), NTH[r] + 1)
                    act.wait_ge(s("h_lo_ready"), 2 * min(B, (GQ * who + 9) // TPB + 2))
                    nc.scalar.activation(h2T[:], ps_m[:], ACT.Copy).then_inc(s("m_freed"), 1)

            def scale_output(g):
                act.wait_ge(s("pv_part"), 4 * (g + 1))
                if g >= 1:
                    act.wait_ge(s("m_filled"), NTH[("G", g - 1, 0)] + 1)
                nc.scalar.activation(oT[:], ps_o[:], ACT.Copy,
                                     scale=mod_a[:, 2, g * GQ // TPB:g * GQ // TPB + 1]).then_inc(s("o_scaled"), 1)

            def attend(i):
                if i >= 9 and (i - 9) % GQ == 0:
                    scale_output((i - 9) // GQ)
                if rounds_of(i, "a"):
                    round_of(rounds_of(i, "a"))
                if i < NT:
                    act.wait_ge(s("max_ready"), i + 1)
                    if i >= 2:
                        act.wait_ge(s("turned"), 2 * (i - 1))
                    nc.scalar.activation(probs[:, i % 2], ps_s[:, i % 2], ACT.Exp, bias=nmax[:, i:i + 1],
                                         accum_out=rsum[:, i:i + 1]).then_inc(s("exp_ready"), 1)
                if 1 <= i <= NT:
                    j = i - 1
                    act.wait_ge(s("turned"), 2 * j + 1)
                    if j // GQ >= 2 and j % GQ == 0:
                        act.wait_ge(s("pv_part"), 4 * (j // GQ - 1))
                    q = j % GQ
                    nc.scalar.activation(pT[:, j // GQ % 2, 0:4, q * P:(q + 1) * P], ps_t[:, 0:4], ACT.Copy).then_inc(s("copied_act"), 1)
                if i == NT + 1:
                    scale_last()
                if rounds_of(i, "b"):
                    round_of(rounds_of(i, "b"))
                if i == ROUTE0:
                    route_exp(0)

            def scale_last():
                scale_output(NG - 1)

            def route_exp(half):
                act.wait_ge(s("route_sub"), half + 1)
                nc.scalar.activation(r_exp[:], r_sub[:], ACT.Exp).then_inc(s("route_exp"), 1)

            def tile(t):
                if 1 <= t <= ALL_TILES:
                    act.wait_ge(s("g_turned"), t)
                    if t >= 3:
                        act.wait_ge(s("y_mm"), t - 2)
                    v = (t - 1) % 2
                    nc.scalar.activation(gT[:, v], ps_t[:, v * 4:v * 4 + 4].rearrange("p a b -> p (a b)"), ACT.Copy).then_inc(s("g_copied"), 1)
                if 0 <= t < ALL_TILES:
                    act.wait_ge(s("hid_biased"), t + 1)
                    if t >= 2:
                        act.wait_ge(s("g_turned"), t - 1)
                    nc.scalar.activation(gl[:, t % 2], hb[:, t % 2], ACT.Gelu_apprx_tanh).then_inc(s("gelu_ready"), 1)

            for n in range(8):
                round_of(("P", 0, n))
            for what, n in ORDER:
                if what == "attend":
                    attend(n)
                if what == "tile":
                    tile(n)
                if what == "route" and n == 1:
                    route_exp(1)

        @block.vector
        def _(dve):
            chain = [0]

            def link(ins):
                chain[0] += 1
                ins.then_inc(s("dve_chain"), 1)
                dve.wait_ge(s("dve_chain"), chain[0])

            def ln1_stats(b, n):
                a = n * GQ
                if n == 0:
                    dve.wait_ge(s("x_loaded"), 16 * (b + 1))
                for t in range(GQ):
                    ins = nc.vector.bn_stats(stats[:, t], x_sb[:, b * TPB + a + t])
                link(ins)
                for t in range(GQ):
                    ins = nc.vector.bn_aggr(mv1[:, a + t], stats[:, t])
                ins.then_inc(s("ln1_stats"), 1)
                dve.wait_ge(s("ln1_stats"), 2 * b + n + 1)

            def ln1_rows(b, n):
                dve.wait_ge(s("rstd1_ready"), 2 * b + n + 1)
                for t in range(n * GQ, (n + 1) * GQ):
                    ins = nc.vector.tensor_scalar(h2[:, b * TPB + t, 0:D], x_sb[:, b * TPB + t], mv1[:, t, 0:1], rstd1[:, t:t + 1],
                                                  ALU.subtract, ALU.mult)
                ins.then_inc(s("z1_ready"), 1)

            def ln2_rows(g):
                dve.wait_ge(s("rstd2_ready"), g + 1)
                b = g * GQ // TPB
                rows = h2[:, g * GQ:(g + 1) * GQ, 0:D]
                for t in range(GQ):
                    ins = nc.vector.tensor_scalar(h2[:, g * GQ + t, 0:D], x_sb[:, g * GQ + t], mv2[:, t, 0:1], rstd2[:, t:t + 1],
                                                  ALU.subtract, ALU.mult)
                link(ins)
                link(nc.vector.tensor_tensor(rows, rows, mod_b[:, b, 1:2].to_broadcast([P, GQ, D]), ALU.mult))
                nc.vector.tensor_tensor(rows, rows, mod_b[:, b, 0:1].to_broadcast([P, GQ, D]), ALU.add).then_inc(s("h2_ready"), 1)

            def clamp(g, sgn):
                link(nc.vector.tensor_scalar(sgn, g, 0.0, 2.0, ALU.is_ge, ALU.mult))
                link(nc.vector.scalar_tensor_tensor(g, g, -1.0, g, ALU.mult, ALU.max))
                link(nc.vector.tensor_scalar(g, g, 0.25, None, ALU.max))
                nc.vector.scalar_tensor_tensor(g, sgn, -1.0, g, ALU.add, ALU.mult).then_inc(s("mod_ready"), 1)

            ln1_stats(0, 0)
            ln1_stats(0, 1)
            dve.wait_ge(s("c_exp_ready"), 1)
            link(nc.vector.tensor_scalar(c_exp[:], c_exp[:], 1.0, None, ALU.add))
            link(nc.vector.reciprocal(c_exp[:], c_exp[:]))
            link(nc.vector.tensor_tensor(c_silu[:], c_exp[:], cT[:], ALU.mult))
            dve.wait_ge(s("const_ready"), 1)
            for b in range(B):
                ins = nc.vector.tensor_scalar(c_rep[:, b], ones[:], c_silu[:, b:b + 1], None, ALU.mult)
            ins.then_inc(s("c_silu_ready"), 1)
            ln1_rows(0, 0)
            ln1_rows(0, 1)
            dve.wait_ge(s("wT_hi_ready"), 1)
            nc.vector.tensor_tensor(wT_lo[:].rearrange("p a b -> p (a b)"), ps_o[:, 0:3 * D],
                                    wT_hi[:].bitcast(F32).rearrange("p a b -> p (a b)"), ALU.subtract).then_inc(s("wT_lo_ready"), 1)
            dve.wait_ge(s("mod_mm"), 1)
            m = ps_t[:, 0, 0:3 * B].rearrange("p (j b) -> p j b", b=B)
            nc.vector.tensor_copy(mod_a[:, 0], m[:, 0])
            nc.vector.tensor_scalar(mod_a[:, 1], m[:, 1], 1.0, None, ALU.add)
            link(nc.vector.tensor_copy(mod_a[:, 2], m[:, 2]))
            clamp(mod_a[:, 2], sgn_a[:])

            def round_of(r):
                kind, who, n = r
                if kind == "P" and n < 2:
                    dve.wait_ge(s("m_filled"), NTH[r] + 1)
                    if 2 * who + n >= 1:
                        dve.wait_ge(s("h_lo_ready"), 2 * who + n)
                    if who >= 1 and n == 0 and ("G", 2 * who - 5, 2) in NTH:
                        dve.wait_ge(s("m_filled"), NTH[("G", 2 * who - 5, 2)] + 1)
                    nc.vector.tensor_scalar(h_f[:], bank_of(r), mod_a[:, 1, who:who + 1], mod_a[:, 0, who:who + 1],
                                            ALU.mult, ALU.add).then_inc(s("m_freed"), 1)
                if kind == "P" and 2 <= n < 6:
                    dve.wait_ge(s("qk_hi"), 4 * who + n - 1)
                    w = (n - 2) // 2
                    t_hi, t_lo = ((q_hi, q_lo), (k_hi, k_lo))[w]
                    col = (n % 2) * 512
                    nc.vector.scalar_tensor_tensor(t_lo[:, who % 2, col:col + 512], bank_of(r), b_cols[:, w:w + 1],
                                                   t_hi[:, who % 2, col:col + 512].bitcast(F32),
                                                   ALU.add, ALU.subtract).then_inc(s("m_freed"), 1)
                if kind == "P" and n >= 6:
                    dve.wait_ge(s("m_filled"), NTH[r] + 1)
                    a = (n - 6) * GQ
                    nc.vector.tensor_tensor(v_sb[:, who % 2, a:a + GQ], bank_of(r).rearrange("p (a b) -> p a b", a=GQ),
                                            bv_bc[:].rearrange("p (o d) -> p o d", o=1).to_broadcast([P, GQ, D]),
                                            ALU.add).then_inc(s("m_freed"), 1)
                if kind == "R":
                    dve.wait_ge(s("m_filled"), NTH[r] + 1)
                    m = ps_m[:, 0:2 * HT * E].rearrange("p (w t e) -> p w t e", w=2, e=E)
                    nc.vector.tensor_copy(pos[:], m[:, 0])
                    nc.vector.tensor_copy(totals[:], m[:, 1].rearrange("p t e -> p e t")).then_inc(s("m_freed"), 1)
                    dve.wait_ge(s("m_freed"), NTH[r] + 1)
                if kind == "M":
                    dve.wait_ge(s("m_filled"), NTH[r] + 1)
                    m = ps_m[:, 0:3 * D].rearrange("p (j f) -> p j f", j=3)
                    nc.vector.tensor_copy(mod_b[:, who, 0], m[:, 0])
                    nc.vector.tensor_scalar(mod_b[:, who, 1], m[:, 1], 1.0, None, ALU.add)
                    nc.vector.tensor_copy(mod_b[:, who, 2], m[:, 2]).then_inc(s("m_freed"), 1)
                    dve.wait_ge(s("m_freed"), NTH[r] + 1)
                    clamp(mod_b[:, who, 2], sgn_b[:])
                    dve.wait_ge(s("mod_ready"), 2 + who)
                if kind == "G" and n == 0:
                    a = who * GQ
                    link(nc.vector.reciprocal(rinv[:, a:a + GQ], rsum[:, a:a + GQ]))
                    dve.wait_ge(s("m_filled"), NTH[r] + 1)
                    for t in range(a, a + GQ):
                        ins = nc.vector.scalar_tensor_tensor(x_sb[:, t], ps_m[:, (t - a) * P:(t - a + 1) * P], rinv[:, t:t + 1],
                                                             x_sb[:, t], ALU.mult, ALU.add)
                    ins.then_inc(s("m_freed"), 1)
                    dve.wait_ge(s("m_freed"), NTH[r] + 1)
                    for t in range(a, a + GQ):
                        ins = nc.vector.bn_stats(stats[:, t - a], x_sb[:, t])
                    link(ins)
                    if who >= 1:
                        dve.wait_ge(s("h2_ready"), who)
                    for t in range(a, a + GQ):
                        ins = nc.vector.bn_aggr(mv2[:, t - a], stats[:, t - a])
                    ins.then_inc(s("ln2_stats"), 1)
                    dve.wait_ge(s("ln2_stats"), who + 1)
                if kind == "G" and n == 2:
                    dve.wait_ge(s("m_filled"), NTH[r] + 1)
                    a = who * GQ
                    nc.vector.tensor_copy(logits[:, a:a + GQ], ps_m[:, 0:GQ * E].rearrange("p (t e) -> p t e", e=E)).then_inc(s("m_freed"), 1)
                    dve.wait_ge(s("m_freed"), NTH[r] + 1)

            def bc_t(ap):
                return ap.rearrange("p (t o) -> p t o", o=1).to_broadcast([P, HT, E])

            def route(half, stage):
                a = half * HT
                lg = logits[:, a:a + HT]
                if stage == 0:
                    link(nc.vector.tensor_reduce(r_max[:], lg, AX.X, ALU.max))
                    nc.vector.tensor_tensor(r_sub[:], lg, bc_t(r_max[:]), ALU.subtract).then_inc(s("route_sub"), 1)
                if stage == 1:
                    dve.wait_ge(s("route_exp"), half + 1)
                    link(nc.vector.tensor_reduce(r_sum[:], r_exp[:], AX.X, ALU.add))
                    link(nc.vector.reciprocal(r_inv[:], r_sum[:]))
                    link(nc.vector.tensor_tensor(r_prob[:], r_exp[:], bc_t(r_inv[:]), ALU.mult))
                    for t in range(HT):
                        ins = nc.vector.max(top_w[:, a + t], r_prob[:, t])
                    link(ins)
                    for t in range(HT):
                        ins = nc.vector.max_index(top_i[:, t], top_w[:, a + t], r_prob[:, t])
                    link(ins)
                if stage == 2:
                    link(nc.vector.tensor_copy(top_f[:], top_i[:, :, 0:TOPK]))
                    nc.vector.tensor_copy(h2[:, a:a + HT, D + 1], top_f[:, :, 1])
                    for k in range(TOPK):
                        ins = nc.vector.tensor_tensor(hot[:, k], iota_e[:].rearrange("p (o e) -> p o e", o=1).to_broadcast([P, HT, E]),
                                                      top_f[:, :, k:k + 1].to_broadcast([P, HT, E]), ALU.is_equal)
                    link(ins)
                    nc.vector.tensor_tensor(hot2[:], hot[:, 0], hot[:, 1], ALU.add).then_inc(s("route_hot"), 1)
                if stage == 3:
                    link(nc.vector.tensor_tensor_scan(upto[:].rearrange("p e t -> p (e t)"), keep[:].rearrange("p e t -> p (e t)"),
                                                      totals[:].rearrange("p e t -> p (e t)"), 0.0, ALU.mult, ALU.add))
                    link(nc.vector.tensor_tensor(cmp_n[:], upto[:, :, HT - 1:HT].to_broadcast([P, E, THR]),
                                            thr[:].rearrange("p (o j) -> p o j", o=1).to_broadcast([P, E, THR]), ALU.is_gt))
                    link(nc.vector.tensor_tensor(upto[:], upto[:], totals[:], ALU.subtract))
                    link(nc.vector.tensor_reduce(n_tiles[:], cmp_n[:], AX.X, ALU.add))
                    link(nc.vector.tensor_tensor_scan(end_t[:], ones[:, 0:E], n_tiles[:], 0.0, ALU.mult, ALU.add))
                    link(nc.vector.tensor_tensor(base_e[:], end_t[:], n_tiles[:], ALU.subtract))
                if stage == 4:
                    link(nc.vector.tensor_scalar(base_e[:], base_e[:], float(P), float(half * TILES * P), ALU.mult, ALU.add))
                    link(nc.vector.tensor_tensor(pos[:], pos[:],
                                                 upto[:].rearrange("p e t -> p t e"), ALU.add))
                    link(nc.vector.tensor_tensor(pos[:], pos[:], base_e[:].rearrange("p (o e) -> p o e", o=1).to_broadcast([P, HT, E]), ALU.add))
                if stage == 5:
                    for k in range(TOPK):
                        ins = nc.vector.tensor_tensor(pos_k[:, k], pos[:], hot[:, k], ALU.mult)
                    link(ins)
                    link(nc.vector.tensor_reduce(slot_f[:], pos_k[:], AX.X, ALU.add))
                    nc.vector.tensor_copy(slot_i[:, half], slot_f[:]).then_inc(s("route_slots"), 1)
                if stage == 6:
                    link(nc.vector.tensor_tensor(cmp_t[:], iota_t[:].rearrange("p (t o) -> p t o", o=1).to_broadcast([P, TILES, E]),
                                                 end_t[:].rearrange("p (o e) -> p o e", o=1).to_broadcast([P, TILES, E]), ALU.is_ge))
                    te = tile_e[:, half * TILES:(half + 1) * TILES]
                    link(nc.vector.tensor_reduce(te, cmp_t[:], AX.X, ALU.add))
                    link(nc.vector.tensor_scalar(te, te, float(E - 1), None, ALU.min))
                    nc.vector.tensor_copy(tile_i[:, half * TILES:(half + 1) * TILES], te).then_inc(s("route_tiles"), 1)
                    dve.wait_ge(s("route_tiles"), half + 1)

            def attend(i):
                if i < NT:
                    dve.wait_ge(s("scores"), i + 1)
                    nc.vector.tensor_reduce(nmax[:, i:i + 1], ps_s[:, i % 2], AX.X, ALU.max, negate=True).then_inc(s("max_ready"), 1)
                if i % TPB in (1, 2) and i // TPB + 1 < B:
                    ln1_rows(i // TPB + 1, i % TPB - 1)
                if rounds_of(i, "a"):
                    round_of(rounds_of(i, "a"))
                if i % TPB < 2 and i // TPB + 1 < B:
                    ln1_stats(i // TPB + 1, i % TPB)
                before_last = rounds_of(i - 1, "b") if i else None
                if before_last and before_last[0] == "G" and before_last[2] == 0:
                    ln2_rows(before_last[1])
                if 1 <= i <= NT:
                    j = i - 1
                    dve.wait_ge(s("turned"), 2 * j + 2)
                    if j // GQ >= 2 and j % GQ == 0:
                        dve.wait_ge(s("pv_part"), 4 * (j // GQ - 1))
                    q = j % GQ
                    nc.vector.tensor_copy(pT[:, j // GQ % 2, 4:8, q * P:(q + 1) * P], ps_t[:, 4:8]).then_inc(s("copied_dve"), 1)
                if rounds_of(i, "b"):
                    round_of(rounds_of(i, "b"))
                if i in W1_STEPS:
                    e = W1_STEPS.index(i)
                    dve.wait_ge(s("w1_loaded"), 16 * (e + 1))
                    link(nc.vector.tensor_copy(w1_hl[:, e, 0], w1_raw[:, e % 2]))
                    nc.vector.tensor_tensor(w1_hl[:, e, 1], w1_raw[:, e % 2], w1_hl[:, e, 0].bitcast(F32),
                                            ALU.subtract).then_inc(s("w1_split"), 1)
                if ROUTE0 <= i < ROUTE0 + 3:
                    for stage in ((0, 1), (2,), (3, 4, 5, 6))[i - ROUTE0]:
                        route(0, stage)

            expert = {}

            def tile(t):
                if 0 <= t < ALL_TILES:
                    if t == 0:
                        dve.wait_ge(s("bias_loaded"), 32)
                    expert[t] = load_expert(dve, t)
                if t + 1 < ALL_TILES:
                    v, w = (t + 1) % 2, (t + 1) % NBUF
                    dve.wait_ge(s("xT_mm"), t + 2)
                    if t >= 1:
                        dve.wait_ge(s("hid_mm"), t)
                    nc.vector.tensor_copy(xT_hi[:, v], ps_x).then_inc(s("xT_hi_ready"), 1)
                    dve.wait_ge(s("xT_hi_ready"), t + 2)
                    nc.vector.tensor_tensor(xT_lo[:, v], ps_x, xT_hi[:, v].bitcast(F32), ALU.subtract).then_inc(s("xT_ready"), 1)
                    nc.vector.tensor_scalar(dst_f[:, t + 1:t + 2], xs[:, w, D + 1:D + 2], tile_e[:, t + 1:t + 2],
                                            xs[:, w, D:D + 1], ALU.is_equal, ALU.add).then_inc(s("dst_ready"), 1)
                if 0 <= t < ALL_TILES:
                    dve.wait_ge(s("hid_mm"), t + 1)
                    if t >= 2:
                        dve.wait_ge(s("gelu_ready"), t - 1)
                    nc.vector.tensor_tensor(hb[:, t % 2], ps_s[:, t % 2, 0:HID], b1_bc[:, bass.ds(expert[t] * HID, HID)],
                                            ALU.add).then_inc(s("hid_biased"), 1)
                if t >= 2:
                    u = (t - 2) % NBUF
                    dve.wait_ge(s("y_mm"), t - 1)
                    if t - 2 >= NBUF:
                        dve.wait_ge(s(f"y_out_{u}"), 16 * ((t - 2) // NBUF))
                    dve.wait_ge(s("dst_ready"), t - 1)
                    nc.vector.tensor_tensor(dst_i[:, u], dst_f[:, t - 2:t - 1], trash[:, t - 2:t - 1], ALU.min)
                    nc.vector.tensor_tensor(y_sb[:, u], ps_y, b2_bc[:, bass.ds(expert.pop(t - 2) * D, D)],
                                            ALU.add).then_inc(s("y_ready"), 1)

            def chunk(n):
                a = n * CHUNK
                dve.wait_ge(s(f"y_in_{n % 4}"), 16 * (n // 4 + 1))
                yc = yy[:, n % 4]
                for t in range(CHUNK):
                    ins = nc.vector.tensor_scalar(yc[:, t, 0:D], yc[:, t, 0:D], top_w[:, a + t, 0:1], None, ALU.mult)
                link(ins)
                for t in range(CHUNK):
                    ins = nc.vector.scalar_tensor_tensor(yc[:, t, 0:D], yc[:, t, D:2 * D], top_w[:, a + t, 1:2], yc[:, t, 0:D], ALU.mult, ALU.add)
                link(ins)
                link(nc.vector.tensor_tensor(yc[:, :, 0:D], yc[:, :, 0:D], mod_b[:, a // TPB, 2:3].to_broadcast([P, CHUNK, D]), ALU.mult))
                nc.vector.tensor_tensor(x_sb[:, a:a + CHUNK], x_sb[:, a:a + CHUNK], yc[:, :, 0:D], ALU.add).then_inc(s("combined"), 1)

            for n in range(8):
                round_of(("P", 0, n))
            for what, n in ORDER:
                if what == "attend":
                    attend(n)
                if what == "tile":
                    tile(n)
                if what == "route":
                    if n == 3:
                        round_of(("R", 1, 0))
                    route(1, n)
                if what == "chunk":
                    chunk(n)

        @block.tensor
        def _(pe):
            def product3(o, l_hi, l_lo, r_hi, r_lo, first=True, last=True):
                nc.tensor.matmul(o, l_hi, r_hi, start=first, stop=False)
                nc.tensor.matmul(o, l_hi, r_lo, start=False, stop=False)
                return nc.tensor.matmul(o, l_lo, r_hi, start=False, stop=last)

            pe.wait_ge(s("w_loaded"), 48)
            pe.wait_ge(s("ident_ready"), 1)
            for w in range(3):
                ins = nc.tensor.transpose(ps_o[:, w * D:(w + 1) * D], w_raw[:, w], ident[:])
            ins.then_inc(s("wT_mm"), 1)
            pe.wait_ge(s("wmod_loaded"), 16)
            pe.wait_ge(s("c_silu_ready"), 1)
            for j in range(3):
                ins = nc.tensor.matmul(ps_t[:, 0, j * B:(j + 1) * B], wmod_sb[:, j], c_silu[:], start=True, stop=True)
            ins.then_inc(s("mod_mm"), 1)

            def round_of(r):
                kind, who, n = r
                if NTH[r] >= 8:
                    pe.wait_ge(s("m_freed"), NTH[r])
                bank = bank_of(r)
                if kind == "P" and n < 2:
                    pe.wait_ge(s("z1_ready"), 2 * who + n + 1)
                    for t in range(GQ):
                        ins = nc.tensor.transpose(bank[:, t * P:(t + 1) * P], h2[:, who * TPB + n * GQ + t, 0:D], ident[:])
                if kind == "P" and 2 <= n < 6:
                    if n == 2:
                        pe.wait_ge(s("h_lo_ready"), 2 * who + 2)
                        if who == 0:
                            pe.wait_ge(s("wT_lo_ready"), 1)
                            pe.wait_ge(s("mod_ready"), 1)
                    w, col = (n - 2) // 2, (n % 2) * 512
                    ins = product3(bank, wT_hi[:, w], wT_lo[:, w], h_hi[:, col:col + 512], h_lo[:, col:col + 512])
                if kind == "P" and n >= 6:
                    for t in range(GQ):
                        a = ((n - 6) * GQ + t) * P
                        ins = product3(bank[:, t * P:(t + 1) * P], h_hi[:, a:a + P], h_lo[:, a:a + P], wT_hi[:, 2], wT_lo[:, 2])
                if kind == "R":
                    pe.wait_ge(s("route_hot"), who + 1)
                    m = hot2[:].rearrange("p t e -> p (t e)")
                    nc.tensor.matmul(ps_m[:, 0:HT * E], before[:], m, start=True, stop=True)
                    ins = nc.tensor.matmul(ps_m[:, HT * E:2 * HT * E], ones[:], m, start=True, stop=True)
                if kind == "M":
                    ins = nc.tensor.matmul(ps_m[:, 0:3 * D], c_rep[:, who], wmod_sb[:, 3:6].rearrange("p a b -> p (a b)"), start=True, stop=True)
                if kind == "G" and n == 0:
                    pe.wait_ge(s("o_scaled"), who + 1)
                    for t in range(GQ):
                        ins = nc.tensor.transpose(ps_m[:, t * P:(t + 1) * P], oT[:, t * P:(t + 1) * P], ident[:])
                if kind == "G" and n == 1:
                    pe.wait_ge(s("h2_ready"), who + 1)
                    for t in range(GQ):
                        ins = nc.tensor.transpose(ps_m[:, t * P:(t + 1) * P], h2[:, who * GQ + t, 0:D], ident[:])
                if kind == "G" and n == 2:
                    for t in range(GQ):
                        ins = nc.tensor.matmul(ps_m[:, t * E:(t + 1) * E], h2T[:, t * P:(t + 1) * P], wr_sb[:], start=True, stop=True)
                ins.then_inc(s("m_filled"), 1)

            def attend(i):
                if i < NT:
                    b = i // TPB
                    if i >= 2:
                        pe.wait_ge(s("exp_ready"), i - 1)
                    if i % TPB == 0:
                        pe.wait_ge(s("m_freed"), NTH[("P", b, 5 if b else 7)] + 1)
                    q = (i % TPB) * P
                    for half in range(2):
                        ins = product3(ps_s[:, i % 2, half * 512:(half + 1) * 512], q_hi[:, b % 2, q:q + P], q_lo[:, b % 2, q:q + P],
                                       k_hi[:, b % 2, half * 512:(half + 1) * 512], k_lo[:, b % 2, half * 512:(half + 1) * 512])
                    ins.then_inc(s("scores"), 1)
                if rounds_of(i, "a"):
                    round_of(rounds_of(i, "a"))
                for g, part in parts_of(i):
                    if part == 0:
                        pe.wait_ge(s("copied_act"), GQ * (g + 1))
                        pe.wait_ge(s("copied_dve"), GQ * (g + 1))
                        pe.wait_ge(s("m_freed"), NTH[("P", g * GQ // TPB, 7)] + 1)
                        if g >= 1:
                            pe.wait_ge(s("o_scaled"), g)
                    for kb in (2 * part, 2 * part + 1):
                        ins = nc.tensor.matmul(ps_o[:], v_sb[:, g * GQ // TPB % 2, kb], pT[:, g % 2, kb], start=(kb == 0), stop=(kb == TPB - 1))
                    ins.then_inc(s("pv_part"), 1)
                if 1 <= i <= NT:
                    j = i - 1
                    pe.wait_ge(s("exp_ready"), j + 1)
                    for h in range(2):
                        if j >= 1:
                            pe.wait_ge(s(("copied_act", "copied_dve")[h]), j)
                        for kb in range(4 * h, 4 * h + 4):
                            ins = nc.tensor.transpose(ps_t[:, kb], probs[:, j % 2, kb * P:(kb + 1) * P], ident[:])
                        ins.then_inc(s("turned"), 1)
                if rounds_of(i, "b"):
                    round_of(rounds_of(i, "b"))

            expert = {}

            def tile(t):
                if t + 1 < ALL_TILES:
                    v = (t + 1) % NBUF
                    pe.wait_ge(s(f"x_in_{v}"), 16 * ((t + 1) // NBUF + 1))
                    if t >= 0:
                        pe.wait_ge(s("xT_ready"), t + 1)
                    nc.tensor.transpose(ps_x, xs[:, v, 0:D], ident[:]).then_inc(s("xT_mm"), 1)
                if t == -1:
                    pe.wait_ge(s("route_tiles"), 1)
                    expert[0] = load_expert(pe, 0)
                if 0 <= t < ALL_TILES:
                    u = t % 2
                    if t == 0:
                        pe.wait_ge(s("w1_split"), E)
                        pe.wait_ge(s("w2_loaded"), 16)
                        pe.wait_ge(s("exp_ready"), NT)
                        pe.wait_ge(s("copied_act"), NT)
                        pe.wait_ge(s("copied_dve"), NT)
                    pe.wait_ge(s("xT_ready"), t + 1)
                    if t >= 2:
                        pe.wait_ge(s("hid_biased"), t - 1)
                    w = w1_hl[:].rearrange("p e a h -> p (e a h)")
                    at = expert[t] * (2 * HID)
                    product3(ps_s[:, u, 0:HID], xT_hi[:, u], xT_lo[:, u], w[:, bass.ds(at, HID)],
                             w[:, bass.ds(at + HID, HID)]).then_inc(s("hid_mm"), 1)
                    if t + 1 < ALL_TILES:
                        if (t + 1) % TILES == 0:
                            pe.wait_ge(s("route_tiles"), (t + 1) // TILES + 1)
                        expert[t + 1] = load_expert(pe, t + 1)
                if 1 <= t <= ALL_TILES:
                    pe.wait_ge(s("gelu_ready"), t)
                    if t >= 3:
                        pe.wait_ge(s("g_copied"), t - 2)
                    v = (t - 1) % 2
                    for j in range(HB):
                        ins = nc.tensor.transpose(ps_t[:, v * 4 + j], gl[:, v, j * P:(j + 1) * P], ident[:])
                    ins.then_inc(s("g_turned"), 1)
                if t >= 2:
                    pe.wait_ge(s("g_copied"), t - 1)
                    if t >= 3:
                        pe.wait_ge(s("y_ready"), t - 2)
                    w = w2_sb[:].rearrange("p e j d -> p (e j d)")
                    at = expert.pop(t - 2) * (HB * D)
                    for j in range(HB):
                        ins = nc.tensor.matmul(ps_y, gT[:, t % 2, j * P:(j + 1) * P],
                                               w[:, bass.ds(at + j * D, D)], start=(j == 0), stop=(j == HB - 1))
                    ins.then_inc(s("y_mm"), 1)

            for n in range(8):
                round_of(("P", 0, n))
            for what, n in ORDER:
                if what == "attend":
                    attend(n)
                if what == "tile":
                    tile(n)
                if what == "route" and n == 2:
                    round_of(("R", 1, 0))


_INS = ['L0_attn_x', 'L0_attn_Wq', 'L0_attn_bq', 'L0_attn_Wk', 'L0_attn_bk', 'L0_attn_Wv', 'L0_attn_bv',
        'L0_ffn_w_router', 'L0_ffn_w1', 'L0_ffn_b1', 'L0_ffn_w2', 'L0_ffn_b2', 'L0_c', 'L0_wmod']


def kernel(**inputs):
    import numpy as _np
    import concourse.bacc as _bacc
    from concourse import mybir as _mybir
    from concourse.bass_utils import run_bass_kernel_spmd as _run

    nc = _bacc.Bacc("TRN2", target_bir_lowering=False, num_devices=1)
    arrays, args = {}, []
    for name in _INS:
        a = _np.ascontiguousarray(inputs[name])
        arrays[f"in_{name}_dram"] = a
        args.append(nc.dram_tensor(f"in_{name}_dram", a.shape, _mybir.dt.from_np(a.dtype), kind="ExternalInput").ap())
    args.append(nc.dram_tensor("out_dram", (B, SEQ, D), F32, kind="ExternalOutput").ap())
    build(nc, *args)
    r = _run(nc, [arrays], core_ids=[0])
    return r.results[0]["out_dram"]
```

```python
from contextlib import ExitStack

import concourse.bass as bass
from concourse import mybir

ALU = mybir.AluOpType
ACT = mybir.ActivationFunctionType
AX = mybir.AxisListType
F32 = mybir.dt.float32
F32R = mybir.dt.float32r
I32 = mybir.dt.int32
U32 = mybir.dt.uint32

P = 128
D = 128
B = 4
SEQ = 1024
TPB = SEQ // P
NT = B * TPB
GQ = 4
NG = NT // GQ
E = 8
HID = 512
HB = HID // P
TOPK = 2
HALVES = 2
HT = NT // HALVES
TILES = (HT * P * TOPK + E * (P - 1)) // P
ROW = D + 2
PAIRS = NT * P * TOPK
NSLOT = HALVES * TILES * P
EPS = 1e-5
THR = HT

ROUNDS_A = {0: ("P", 7), 2: ("G", 2), 3: ("P", 1), 4: ("P", 2), 5: ("P", 4), 6: ("P", 5), 7: ("P", 6)}
ROUNDS_B = {1: ("G", 1), 2: ("P", 0), 4: ("P", 3), 5: ("G", 1), 6: ("G", 2)}
G_STEP = {1: 9, 2: 10}
X1_STEP = 4
GATE_A_STEP, GATE_B_STEP = X1_STEP - 1, X1_STEP + 1
MODS = {(0, "a"): 0, (1, "a"): 1, (1, "b"): 2, (2, "a"): 3}
ROUTE0 = GQ * (NG // 2 - 1) + G_STEP[2]
MOVED = {(ROUTE0 + 1, "b"): ("R", 0, 0)}
LATE_NORM = ROUTE0 + 2
TAIL = {NT + 1: (None, ("G", NG - 2, 1)), NT + 2: (("G", NG - 2, 2), None),
        NT + 3: (None, ("G", NG - 1, 1)), NT + 4: (None, ("G", NG - 1, 2))}
STEPS = NT + 6
NBUF = 6
YBUF = 16
YSEM = 4
YRUN = YBUF // YSEM
ALL_TILES = HALVES * TILES
CHUNK = 4
NCHUNK = NT // CHUNK
CHOICE_AFTER = {1: 1, NG // 2 - 1: 1, NG - 3: 1, NG - 2: 1, NG - 1: 1}
POOL_GROUPS = NG // 2
ROUTE1 = STEPS - NT - 2
SCATTERS = HT * TOPK
SCATTER0 = {ROUTE0 + 2 + n: m for n, m in enumerate((3, 3, 4, 4, 5, 5, 4, 4))}
SCATTER1 = ROUTE1 + 3
SCATTER1_TILES = TILES - 4 - SCATTER1


def rounds_of(i, where):
    if i > NT:
        return TAIL.get(i, (None, None))["ab".index(where)]
    if (i, where) in MOVED:
        return MOVED[i, where]
    if (i, where) in MODS:
        return ("M", MODS[i, where], 0)
    r = (ROUNDS_A if where == "a" else ROUNDS_B).get(i % TPB)
    if r is None:
        return None
    kind, n = r
    if kind == "P":
        b = i // TPB + (0 if n == 7 else 1)
        return ("P", b, n) if 1 <= b < B else None
    first = i - G_STEP[n]
    return ("G", first // GQ, n) if first >= 0 and first % GQ == 0 else None


def logits_step(g):
    return [i for i in range(STEPS) for w in "ab" if rounds_of(i, w) == ("G", g, 2)][0]


def ln1_of(i):
    if i == 0:
        return (1, 0)
    b, n = {7: (2, 0), 1: (1, 1)}.get(i % TPB, (B, 0))
    return (i // TPB + b, n) if i // TPB + b < B else None


def products_of(i):
    if i >= NT - 1:
        return {NT - 1: [NT - 4, NT - 3], NT: [NT - 2], NT + 1: [NT - 1]}.get(i, [])
    return [i - 3] if i >= 3 else []


def sums_of(i):
    if i >= NT:
        return {NT: [NT - 4, NT - 3], NT + 1: [NT - 2, NT - 1]}.get(i, [])
    return [i - X1_STEP] if i >= X1_STEP else []


def summed(i):
    last = max(sums_of(i), default=0)
    return last // GQ if last % GQ == GQ - 1 else None


def all_rounds():
    order = [("P", 0, n) for n in range(8)]
    for i in range(STEPS):
        order += [r for r in (rounds_of(i, "a"), rounds_of(i, "b")) if r]
    return order + [("R", 1, 0)]


def schedule():
    order = [("attend", i) for i in range(NT + 2)]
    order += [("tile", -2), ("tile", -1), ("attend", NT + 2), ("tile", 0), ("tile", 1), ("attend", NT + 3)]
    for i in range(NT + 4, STEPS):
        order += [("tile", i - NT - 2), ("attend", i)]
    for t in range(ROUTE1, ALL_TILES + 1):
        order.append(("tile", t))
        if 0 <= t - ROUTE1 < 4:
            order.append(("route", t - ROUTE1))
        n, rest = divmod((t - TILES - 15) * 2, 3)
        if rest < 2 and 0 <= n < HT:
            order.append(("weigh", (n, 1)))
        if rest < 2 and 1 <= n <= HT:
            order.append(("combine", (n - 1, 1)))
    for a in range(HT, NT, CHUNK):
        order += [("weigh", (a, CHUNK)), ("combine", (a, CHUNK))]
    return order


def build(nc, x, Wq, bq, Wk, bk, Wv, bv, w_router, w1, b1, w2, b2, c, wmod, out):
    NTH = {r: n for n, r in enumerate(all_rounds())}
    ORDER = schedule()

    with ExitStack() as ctx:
        def sb(name, shape, dt=F32):
            return ctx.enter_context(nc.sbuf_tensor(name, shape, dt))

        def sem(name):
            return ctx.enter_context(nc.semaphore(name))

        ps_s = ctx.enter_context(nc.psum_tensor("ps_s", [P, 2, SEQ], F32))
        ps_t = ctx.enter_context(nc.psum_tensor("ps_t", [P, TPB, P], F32))
        ps_o = ctx.enter_context(nc.psum_tensor("ps_o", [P, GQ * P], F32))
        ps_m = ctx.enter_context(nc.psum_tensor("ps_m", [P, GQ * P], F32))

        ident = sb("ident", [P, P])
        before = sb("before", [P, P])
        ones = sb("ones", [P, P])
        iota_e = sb("iota_e", [P, E])
        iota_t = sb("iota_t", [P, TILES])
        thr = sb("thr", [P, THR])
        keep = sb("keep", [P, E, HT])
        trash = sb("trash", [P, HALVES * TILES])

        x_sb = sb("x_sb", [P, NT, D])
        wT_hi = sb("wT_hi", [P, 2, D], F32R)
        wT_lo = sb("wT_lo", [P, 2, D], F32R)
        b_cols = sb("b_cols", [P, 2])
        bv_bc = sb("bv_bc", [P, D])
        cT = sb("cT", [P, B])
        c_exp = sb("c_exp", [P, B])
        c_silu = sb("c_silu", [P, B])
        mod_a = sb("mod_a", [P, 2, B])
        mod_b = sb("mod_b", [P, B, 4, D])
        wr_sb = sb("wr_sb", [P, E])

        stats = sb("stats", [P, GQ, 6])
        mv1 = sb("mv1", [P, TPB, 2])
        stats2 = sb("stats2", [P, GQ, 6])
        mv2 = sb("mv2", [P, 2, GQ, 2])
        var1 = sb("var1", [P, TPB])
        var2 = sb("var2", [P, GQ])
        mhalf = sb("mhalf", [P, GQ])
        rstd1 = sb("rstd1", [P, TPB])
        rstd2 = sb("rstd2", [P, GQ])
        h_f = sb("h_f", [P, 2, GQ * P])
        h_hi = sb("h_hi", [P, SEQ], F32R)
        h_lo = sb("h_lo", [P, SEQ], F32R)
        q_hi = sb("q_hi", [P, 2, SEQ], F32R)
        q_lo = sb("q_lo", [P, 2, SEQ], F32R)
        k_hi = sb("k_hi", [P, 2, SEQ], F32R)
        k_lo = sb("k_lo", [P, 2, SEQ], F32R)
        v_sb = sb("v_sb", [P, 2, TPB, D])
        nmax = sb("nmax", [P, NT])
        rsum = sb("rsum", [P, NT])
        rinv = sb("rinv", [P, NT])
        probs = sb("probs", [P, 2, SEQ])
        pT = sb("pT", [P, 2, TPB, GQ * P])
        early = pT[:, 1].rearrange("p a b -> p (a b)")
        w_raw = early[:, 0:3 * D].rearrange("p (w d) -> p w d", w=3)
        wmod_sb = early[:, 3 * D:9 * D].rearrange("p (j f) -> p j f", j=6)
        c_rep = early[:, 9 * D:(9 + B) * D].rearrange("p (b f) -> p b f", b=B)
        o_gated = sb("o_gated", [P, GQ, D])
        h2 = sb("h2", [P, NT, ROW])
        logits = sb("logits", [P, NT, E])

        r_max = sb("r_max", [P, GQ])
        r_sub = sb("r_sub", [P, GQ, E])
        r_exp = sb("r_exp", [P, GQ, E])
        r_sum = sb("r_sum", [P, GQ])
        r_inv = sb("r_inv", [P, GQ])
        r_prob = sb("r_prob", [P, GQ, E])
        top_w = sb("top_w", [P, NT, 8])
        top_i = sb("top_i", [P, GQ, 8], U32)
        top_f = sb("top_f", [P, HT, TOPK])
        hot = sb("hot", [P, TOPK, HT, E])
        hot2 = sb("hot2", [P, HT, E])
        totals = sb("totals", [P, E, HT])
        upto = sb("upto", [P, E, HT])
        cmp_n = sb("cmp_n", [P, E, THR])
        n_tiles = sb("n_tiles", [P, E])
        end_t = sb("end_t", [P, E])
        base_e = sb("base_e", [P, E])
        pos = sb("pos", [P, HT, E])
        pos_k = sb("pos_k", [P, TOPK, HT, E])
        slot_f = sb("slot_f", [P, TOPK, HT])
        slot_i = sb("slot_i", [P, HALVES, TOPK, HT], I32)
        cmp_t = sb("cmp_t", [P, TILES, E])
        tile_e = sb("tile_e", [P, HALVES * TILES])
        tile_i = sb("tile_i", [P, HALVES * TILES], I32)

        w1_sb = sb("w1_sb", [P, E, HID])
        w2_sb = sb("w2_sb", [P, E, HB, D])
        b1_cols = sb("b1_cols", [P, E * HB])
        b2_bc = sb("b2_bc", [P, E * D])
        w1_t = sb("w1_t", [P, 3, HID])
        b1_t = sb("b1_t", [P, 3, HB])
        blank = sb("blank", [P, ROW])
        xs = sb("xs", [P, NBUF, ROW])
        xT = sb("xT", [P, 3, P])
        gT = probs[:, :, 0:HID]
        yy = pT[:, 1].rearrange("p a b -> p (a b)").rearrange("p (n t kd) -> p n t kd", n=4, t=CHUNK)
        y_sb = sb("y_sb", [P, YBUF, D])
        sgn_b = y_sb[:, 0:B]
        wvT = y_sb[:, B]
        h2T = y_sb[:, YBUF - GQ:].rearrange("p a b -> p (a b)")
        dst_f = sb("dst_f", [P, HALVES * TILES])
        dst_i = sb("dst_i", [P, YBUF, 1], I32)
        slots_dram = nc.dram_tensor("slots", (NSLOT, ROW), F32, kind="Internal").ap()
        y_dram = nc.dram_tensor("pairs", (PAIRS + NSLOT, D), F32, kind="Internal").ap()

        S = {n: sem(n) for n in (
            "ident_ready w_loaded x_loaded c_loaded qkv_bias_loaded router_loaded c_rep_ready wmod_loaded "
            "w1_loaded w2_loaded bias_loaded "
            "mod_mm mod_ready c_exp_ready c_silu_ready wT_mm wT_hi_ready wT_lo_ready "
            "var1_ready rstd1_ready var2_ready rstd2_ready z1_ready z2_ready dve_chain pool_chain "
            "m_filled m_freed h_hi_ready h_lo_ready qk_hi "
            "scores max_ready exp_ready turned copied output_ready o_taken sum_made h2_ready "
            "choice_sub choice_exp choice_made route_slots route_tiles blank_ready "
            "slots_blank scattered_0 scattered_1 x_in_0 x_in_1 x_in_2 x_in_3 x_in_4 x_in_5 "
            "xT_mm xT_ready hid_mm tile_weights gelu_ready "
            "y_mm y_ready dst_ready y_out_0 y_out_1 y_out_2 y_out_3 y_in_0 y_in_1 y_in_2 y_in_3 "
            "weighed gated combined out_done").split()}

        def s(name):
            return S[name]

        x_t = x.rearrange("b (t p) d -> p (b t) d", p=P)
        out_t = out.rearrange("b (t p) d -> p (b t) d", p=P)
        y_pairs = y_dram[0:PAIRS].rearrange("(t p k) d -> p t (k d)", p=P, k=TOPK)
        def ps_h(t):
            return ps_s[:, t % 2, 0:HID]

        def ps_x(t):
            return ps_s[:, t % 2, 512:512 + P]

        def ps_y(t):
            return ps_t[:, t % 2 * 4]

        def bank_of(r):
            kind, who, n = r
            if kind != "P" or who or n == 0:
                return ps_m[:]
            if n <= 4:
                return ps_s[:, (n - 1) // 2, (n - 1) % 2 * 512:(n - 1) % 2 * 512 + 512]
            return {5: ps_t[:, 4:8].rearrange("p a b -> p (a b)"), 6: ps_o[:],
                    7: ps_t[:, 0:4].rearrange("p a b -> p (a b)")}[n]

        def load_expert(eng, t):
            return eng.value_load(tile_i[0:1, t:t + 1], min_val=0, max_val=E - 1)

        block = ctx.enter_context(nc.Block())

        @block.sync
        def _(sp):
            for b in range(B):
                sp.dma_start(x_sb[:, b * TPB:(b + 1) * TPB], x_t[:, b * TPB:(b + 1) * TPB]).then_inc(s("x_loaded"), 16)
                if b == 0:
                    for h, w in enumerate((Wq, Wk, Wv)):
                        sp.dma_start(w_raw[:, h], w).then_inc(s("w_loaded"), 16)
                    sp.dma_start(wmod_sb, wmod.rearrange("k (j f) -> k j f", j=6)).then_inc(s("wmod_loaded"), 16)
                    sp.dma_start(b_cols[:, 0:1], bq.rearrange("(d o) -> d o", o=1)).then_inc(s("qkv_bias_loaded"), 16)
                    sp.dma_start(b_cols[:, 1:2], bk.rearrange("(d o) -> d o", o=1)).then_inc(s("qkv_bias_loaded"), 16)
                    sp.dma_start(bv_bc[:], bv.rearrange("(o d) -> o d", o=1).to_broadcast([P, D])).then_inc(s("qkv_bias_loaded"), 16)
                    sp.dma_start(wr_sb[:], w_router).then_inc(s("router_loaded"), 16)
                sp.wait_ge(s("x_loaded"), 16 * (b + 1))
            sp.dma_start(w2_sb[:], w2.rearrange("e (j p) d -> p e j d", p=P)).then_inc(s("w2_loaded"), 16)
            sp.wait_ge(s("blank_ready"), 1)
            sp.dma_start(slots_dram.rearrange("(p t) r -> p t r", p=P),
                         blank[:].rearrange("p (o r) -> p o r", o=1).to_broadcast([P, ALL_TILES, ROW])).then_inc(s("slots_blank"), 16)
            sp.dma_start(w1_sb[:], w1.rearrange("e k h -> k e h")).then_inc(s("w1_loaded"), 16)
            sp.dma_start(b2_bc[:], b2.rearrange("(o e) d -> o (e d)", o=1).to_broadcast([P, E * D])).then_inc(s("bias_loaded"), 16)
            sp.dma_start(b1_cols[:], b1.rearrange("e (j p) -> p (e j)", p=P), allow_slow_non_contiguous=True).then_inc(s("bias_loaded"), 16)

            def load_tile(t):
                if t % TILES == 0:
                    sp.wait_ge(s(f"scattered_{t // TILES}"), 16 * TOPK * HT)
                if t >= NBUF:
                    sp.wait_ge(s("xT_mm"), t - NBUF + 1)
                    sp.wait_ge(s("dst_ready"), t - NBUF + 1)
                sp.dma_start(xs[:, t % NBUF], slots_dram[t * P:(t + 1) * P]).then_inc(s(f"x_in_{t % NBUF}"), 16)

            def load_pairs(half):
                end = min(-(-(half + 1) * TILES // YRUN) * YRUN, ALL_TILES)
                for r in range(YSEM):
                    sp.wait_ge(s(f"y_out_{r}"), 16 * len([t for t in range(end) if t // YRUN % YSEM == r]))
                for n in range(4):
                    if half:
                        sp.wait_ge(s("combined"), CHUNK * (n + 1))
                    else:
                        sp.wait_ge(s("output_ready"), NT)
                    a = half * HT + n * CHUNK
                    sp.dma_start(yy[:, n], y_pairs[:, a:a + CHUNK]).then_inc(s(f"y_in_{n}"), 16)

            def store(n):
                sp.wait_ge(s("combined"), CHUNK * (n + 1) if n < NCHUNK // HALVES else HT + n + 1 - NCHUNK // HALVES)
                sp.dma_start(out_t[:, n * CHUNK:(n + 1) * CHUNK], x_sb[:, n * CHUNK:(n + 1) * CHUNK]).then_inc(s("out_done"), 16)

            for t in range(NBUF - 1):
                load_tile(t)
            for what, n in ORDER:
                if what == "tile" and 0 <= n < ALL_TILES - NBUF + 1:
                    load_tile(n + NBUF - 1)
                if what == "tile" and n == TILES + 12:
                    load_pairs(0)
                if what == "combine" and n[0] < HT and n[0] % CHUNK == CHUNK - 1:
                    store(n[0] // CHUNK)
            load_pairs(1)
            for n in range(NCHUNK // HALVES, NCHUNK):
                store(n)
            sp.wait_ge(s("out_done"), 16 * NCHUNK)

        @block.gpsimd
        def _(pool):
            chain = [0]

            def link(ins):
                chain[0] += 1
                ins.then_inc(s("pool_chain"), 1)
                pool.wait_ge(s("pool_chain"), chain[0])

            nc.gpsimd.memset(ident[:], 0.0).then_inc(s("pool_chain"), 1)
            nc.gpsimd.memset(before[:], 0.0).then_inc(s("pool_chain"), 1)
            nc.gpsimd.memset(ones[:], 1.0).then_inc(s("pool_chain"), 1)
            nc.gpsimd.memset(keep[:], 1.0).then_inc(s("pool_chain"), 1)
            chain[0] = 4
            pool.wait_ge(s("pool_chain"), 4)
            nc.gpsimd.affine_select(out=ident[:], in_=ident[:], compare_op=ALU.not_equal, fill=1.0, base=0,
                                    pattern=[[-1, P]], channel_multiplier=1).then_inc(s("ident_ready"), 1)
            nc.gpsimd.affine_select(out=before[:], in_=before[:], compare_op=ALU.is_ge, fill=1.0, base=0,
                                    pattern=[[-1, P]], channel_multiplier=1)
            nc.gpsimd.memset(keep[:, :, 0:1], 0.0)
            f = dict(allow_small_or_imprecise_dtypes=True)
            nc.gpsimd.iota(iota_e[:], [[1, E]], base=0, channel_multiplier=0, **f)
            nc.gpsimd.iota(iota_t[:], [[1, TILES]], base=0, channel_multiplier=0, **f)
            nc.gpsimd.iota(thr[:], [[P, THR]], base=0, channel_multiplier=0, **f)
            nc.gpsimd.iota(trash[:], [[P, HALVES * TILES]], base=PAIRS, channel_multiplier=1, **f)
            nc.gpsimd.iota(h2[:, :, D:D + 1], [[TOPK * P, NT], [1, 1]], base=0, channel_multiplier=TOPK, **f)
            link(nc.gpsimd.memset(blank[:], 0.0))
            link(nc.gpsimd.memset(blank[:, D:D + 1], 1e6))
            link(nc.gpsimd.memset(mhalf[:], -0.5))
            nc.gpsimd.memset(blank[:, D + 1:D + 2], -1.0).then_inc(s("blank_ready"), 1)

            def power(rstd, var):
                return nc.gpsimd.tensor_tensor(rstd, var, mhalf[:], ALU.pow)

            def rstd1_of(b, n):
                pool.wait_ge(s("var1_ready"), 2 * b + n + 1)
                power(rstd1[:, n * GQ:(n + 1) * GQ], var1[:, n * GQ:(n + 1) * GQ]).then_inc(s("rstd1_ready"), 1)

            def rstd2_of(g):
                pool.wait_ge(s("var2_ready"), g + 1)
                power(rstd2[:], var2[:]).then_inc(s("rstd2_ready"), 1)

            def modulate(g):
                pool.wait_ge(s("z2_ready"), g + 1)
                rows = h2[:, g * GQ:(g + 1) * GQ, 0:D]
                b = g * GQ // TPB
                link(nc.gpsimd.tensor_tensor(rows, rows, mod_b[:, b, 2:3].to_broadcast([P, GQ, D]), ALU.mult))
                nc.gpsimd.tensor_tensor(rows, rows, mod_b[:, b, 1:2].to_broadcast([P, GQ, D]), ALU.add).then_inc(s("h2_ready"), 1)

            def h_low(b, n):
                k = 2 * b + n
                pool.wait_ge(s("h_hi_ready"), k + 1)
                nc.gpsimd.tensor_tensor(h_lo[:, n * 512:(n + 1) * 512], h_f[:, n], h_hi[:, n * 512:(n + 1) * 512].bitcast(F32),
                                        ALU.subtract).then_inc(s("h_lo_ready"), 1)

            def scatter(half, a, n):
                for m in range(a, min(a + n, SCATTERS)):
                    if m == 0:
                        pool.wait_ge(s("route_slots"), half + 1)
                        if half == 0:
                            pool.wait_ge(s("slots_blank"), 16)
                    t, k = divmod(m, TOPK)
                    nc.gpsimd.indirect_dma_start(
                        out=slots_dram, out_offset=bass.IndirectOffsetOnAxis(ap=slot_i[:, half, k, t:t + 1], axis=0),
                        in_=h2[:, half * HT + t], in_offset=None).then_inc(s(f"scattered_{half}"), 16)

            def attend(i):
                if i in SCATTER0:
                    scatter(0, sum(n for j, n in SCATTER0.items() if j < i), SCATTER0[i])
                if summed(i - 1) is not None and summed(i - 1) < POOL_GROUPS:
                    modulate(summed(i - 1))
                if ln1_of(i):
                    rstd1_of(*ln1_of(i))
                for where in "ab":
                    r = rounds_of(i, where)
                    if r and r[0] == "P" and r[2] < 2:
                        h_low(r[1], r[2])
                if summed(i) is not None:
                    rstd2_of(summed(i))

            def send(t):
                u = t % YBUF
                pool.wait_ge(s("y_ready"), t + 1)
                nc.gpsimd.indirect_dma_start(
                    out=y_dram, out_offset=bass.IndirectOffsetOnAxis(ap=dst_i[:, u, 0:1], axis=0),
                    in_=y_sb[:, u], in_offset=None).then_inc(s(f"y_out_{u // YRUN}"), 16)

            rstd1_of(0, 0)
            rstd1_of(0, 1)
            sent = 0
            for what, n in ORDER:
                if what == "attend":
                    attend(n)
                if what == "combine" and n[1] == CHUNK:
                    a = n[0]
                    pool.wait_ge(s("gated"), (a - HT) // CHUNK + 1)
                    yc = yy[:, a // CHUNK % 4]
                    nc.gpsimd.tensor_tensor(x_sb[:, a:a + CHUNK], x_sb[:, a:a + CHUNK], yc[:, :, 0:D], ALU.add).then_inc(s("combined"), 1)
                if what == "tile" and n >= 1:
                    if SCATTER1 <= n < SCATTER1 + SCATTER1_TILES:
                        a, z = ((n - SCATTER1 + m) * SCATTERS // SCATTER1_TILES for m in (0, 1))
                        scatter(1, a, z - a)
                        now = sent + (1 if (n - SCATTER1) % 5 in (0, 2, 4) else 0)
                    else:
                        now = min(sent + 2, n)
                    for t in range(sent, now):
                        send(t)
                    sent = now

        @block.scalar
        def _(act):
            act.dma_start(cT[:], c.rearrange("b k -> k b"), allow_slow_non_contiguous=True).then_inc(s("c_loaded"), 16)
            act.wait_ge(s("c_loaded"), 16)
            nc.scalar.activation(c_exp[:], cT[:], ACT.Exp, scale=-1.0).then_inc(s("c_exp_ready"), 1)
            act.wait_ge(s("wT_mm"), 1)
            nc.scalar.activation(wvT, ps_o[:, 2 * D:3 * D], ACT.Copy)
            nc.scalar.activation(wT_hi[:].rearrange("p a b -> p (a b)"), ps_o[:, 0:2 * D], ACT.Copy).then_inc(s("wT_hi_ready"), 1)

            def round_of(r):
                kind, who, n = r
                if kind == "P" and n < 2:
                    act.wait_ge(s("m_freed"), NTH[r] + 1)
                    if who >= 1:
                        act.wait_ge(s("m_filled"), NTH[("P", who - 1, 7)] + 1)
                    nc.scalar.activation(h_hi[:, n * 512:(n + 1) * 512], h_f[:, n], ACT.Copy).then_inc(s("h_hi_ready"), 1)
                if kind == "P" and 2 <= n < 6:
                    act.wait_ge(s("m_filled"), NTH[r] + 1)
                    if who == 0 and n == 2:
                        act.wait_ge(s("qkv_bias_loaded"), 48)
                    t_hi = (q_hi, k_hi)[(n - 2) // 2]
                    col = (n % 2) * 512
                    nc.scalar.activation(t_hi[:, who % 2, col:col + 512], bank_of(r), ACT.Identity,
                                         bias=b_cols[:, (n - 2) // 2:(n - 2) // 2 + 1]).then_inc(s("qk_hi"), 1)
                if kind == "M":
                    act.wait_ge(s("m_filled"), NTH[r] + 1)
                    nc.scalar.activation(mod_b[:, who].rearrange("p j f -> p (j f)"), ps_m[:], ACT.Copy).then_inc(s("m_freed"), 1)
                if kind == "G" and n == 1:
                    act.wait_ge(s("m_filled"), NTH[r] + 1)
                    nc.scalar.activation(h2T, ps_m[:], ACT.Copy).then_inc(s("m_freed"), 1)

            def attend(i):
                if rounds_of(i, "a"):
                    round_of(rounds_of(i, "a"))
                if i < NT:
                    act.wait_ge(s("max_ready"), i + 1)
                    if i >= 2:
                        act.wait_ge(s("turned"), i - 1)
                    nc.scalar.activation(probs[:, i % 2], ps_s[:, i % 2], ACT.Exp, bias=nmax[:, i:i + 1],
                                         accum_out=rsum[:, i:i + 1]).then_inc(s("exp_ready"), 1)
                if rounds_of(i, "b"):
                    round_of(rounds_of(i, "b"))
                if 1 <= i <= NT:
                    j = i - 1
                    act.wait_ge(s("turned"), j + 1)
                    if j // GQ >= 2 and j % GQ == 0:
                        act.wait_ge(s("output_ready"), 4 * (j // GQ - 1))
                    q = j % GQ
                    nc.scalar.activation(pT[:, j // GQ % 2, :, q * P:(q + 1) * P], ps_t[:], ACT.Copy).then_inc(s("copied"), 1)
                for where in "ab":
                    r = rounds_of(i, where)
                    if r and r[0] == "G" and r[2] == 2:
                        choice_exp(r[1])

            def choice_exp(g):
                act.wait_ge(s("choice_sub"), g + 1)
                nc.scalar.activation(r_exp[:], r_sub[:], ACT.Exp).then_inc(s("choice_exp"), 1)

            def tile(t):
                if 0 <= t < ALL_TILES:
                    act.wait_ge(s("tile_weights"), t + 1)
                    act.wait_ge(s("hid_mm"), t + 1)
                    if t >= 2:
                        act.wait_ge(s("y_mm"), t - 1)
                    for j in range(HB):
                        ins = nc.scalar.activation(gT[:, t % 2, j * P:(j + 1) * P], ps_h(t)[:, j * P:(j + 1) * P],
                                                   ACT.Gelu_apprx_tanh, bias=b1_t[:, t % 3, j:j + 1])
                    ins.then_inc(s("gelu_ready"), 1)

            def weigh(a, n):
                c = a // CHUNK
                if a % CHUNK == 0:
                    act.wait_ge(s(f"y_in_{c % 4}"), 16 * (c // 4 + 1))
                for t in range(a, a + n):
                    for k in range(TOPK):
                        y = yy[:, c % 4, t % CHUNK, k * D:(k + 1) * D]
                        if k == 0 or n == 1:
                            ins = nc.scalar.activation(y, y, ACT.Copy, scale=top_w[:, t, k:k + 1])
                ins.then_inc(s("weighed"), 1)

            for n in range(8):
                round_of(("P", 0, n))
            for what, n in ORDER:
                if what == "attend":
                    attend(n)
                if what == "tile":
                    tile(n)
                if what == "weigh":
                    weigh(*n)

        @block.vector
        def _(dve):
            chain = [0]

            def link(ins):
                chain[0] += 1
                ins.then_inc(s("dve_chain"), 1)
                dve.wait_ge(s("dve_chain"), chain[0])

            def ln1_stats(b, n):
                a = n * GQ
                if n == 0:
                    dve.wait_ge(s("x_loaded"), 16 * (b + 1))
                for t in range(GQ):
                    ins = nc.vector.bn_stats(stats[:, t], x_sb[:, b * TPB + a + t])
                link(ins)
                for t in range(GQ):
                    ins = nc.vector.bn_aggr(mv1[:, a + t], stats[:, t])
                link(ins)
                nc.vector.tensor_scalar(var1[:, a:a + GQ], mv1[:, a:a + GQ, 1], EPS, None, ALU.add).then_inc(s("var1_ready"), 1)

            def ln1_rows(b, n):
                dve.wait_ge(s("rstd1_ready"), 2 * b + n + 1)
                for t in range(n * GQ, (n + 1) * GQ):
                    ins = nc.vector.tensor_scalar(h2[:, b * TPB + t, 0:D], x_sb[:, b * TPB + t], mv1[:, t, 0:1], rstd1[:, t:t + 1],
                                                  ALU.subtract, ALU.mult)
                ins.then_inc(s("z1_ready"), 1)

            def ln2_rows(g):
                dve.wait_ge(s("rstd2_ready"), g + 1)
                b = g * GQ // TPB
                rows = h2[:, g * GQ:(g + 1) * GQ, 0:D]
                for t in range(GQ):
                    ins = nc.vector.tensor_scalar(h2[:, g * GQ + t, 0:D], x_sb[:, g * GQ + t], mv2[:, g % 2, t, 0:1], rstd2[:, t:t + 1],
                                                  ALU.subtract, ALU.mult)
                if g < POOL_GROUPS:
                    ins.then_inc(s("z2_ready"), 1)
                    return
                link(ins)
                link(nc.vector.tensor_tensor(rows, rows, mod_b[:, b, 2:3].to_broadcast([P, GQ, D]), ALU.mult))
                nc.vector.tensor_tensor(rows, rows, mod_b[:, b, 1:2].to_broadcast([P, GQ, D]), ALU.add).then_inc(s("h2_ready"), 1)

            def clamp(g, sgn):
                link(nc.vector.tensor_scalar(sgn, g, 0.0, 2.0, ALU.is_ge, ALU.mult))
                link(nc.vector.scalar_tensor_tensor(g, g, -1.0, g, ALU.mult, ALU.max))
                link(nc.vector.tensor_scalar(g, g, 0.25, None, ALU.max))
                nc.vector.scalar_tensor_tensor(g, sgn, -1.0, g, ALU.add, ALU.mult).then_inc(s("mod_ready"), 1)

            ln1_stats(0, 0)
            dve.wait_ge(s("c_exp_ready"), 1)
            link(nc.vector.tensor_scalar(c_exp[:], c_exp[:], 1.0, None, ALU.add))
            link(nc.vector.reciprocal(c_exp[:], c_exp[:]))
            nc.vector.tensor_tensor(c_silu[:], c_exp[:], cT[:], ALU.mult).then_inc(s("c_silu_ready"), 1)
            ln1_stats(0, 1)
            ln1_rows(0, 0)
            ln1_rows(0, 1)
            dve.wait_ge(s("mod_mm"), 1)
            m = ps_t[:, 0, 0:2 * B].rearrange("p (j b) -> p j b", b=B)
            nc.vector.tensor_copy(mod_a[:, 0], m[:, 0])
            nc.vector.tensor_scalar(mod_a[:, 1], m[:, 1], 1.0, None, ALU.add).then_inc(s("mod_ready"), 1)
            dve.wait_ge(s("mod_ready"), 1)

            def round_of(r):
                kind, who, n = r
                if kind == "P" and n < 2:
                    dve.wait_ge(s("m_filled"), NTH[r] + 1)
                    if who >= 1:
                        dve.wait_ge(s("h_lo_ready"), 2 * who + n - 1)
                    nc.vector.tensor_scalar(h_f[:, n], bank_of(r), mod_a[:, 1, who:who + 1], mod_a[:, 0, who:who + 1],
                                            ALU.mult, ALU.add).then_inc(s("m_freed"), 1)
                if kind == "P" and 2 <= n < 6:
                    if who == 0 and n == 2:
                        dve.wait_ge(s("qkv_bias_loaded"), 48)
                    dve.wait_ge(s("qk_hi"), 4 * who + n - 1)
                    w = (n - 2) // 2
                    t_hi, t_lo = ((q_hi, q_lo), (k_hi, k_lo))[w]
                    col = (n % 2) * 512
                    nc.vector.scalar_tensor_tensor(t_lo[:, who % 2, col:col + 512], bank_of(r), b_cols[:, w:w + 1],
                                                   t_hi[:, who % 2, col:col + 512].bitcast(F32),
                                                   ALU.add, ALU.subtract).then_inc(s("m_freed"), 1)
                if kind == "P" and n >= 6:
                    dve.wait_ge(s("m_filled"), NTH[r] + 1)
                    a = (n - 6) * GQ
                    nc.vector.tensor_tensor(v_sb[:, who % 2, a:a + GQ], bank_of(r).rearrange("p (a b) -> p a b", a=GQ),
                                            bv_bc[:].rearrange("p (o d) -> p o d", o=1).to_broadcast([P, GQ, D]),
                                            ALU.add).then_inc(s("m_freed"), 1)
                if kind == "R":
                    dve.wait_ge(s("m_filled"), NTH[r] + 1)
                    m = ps_m[:, 0:2 * HT * E].rearrange("p (w t e) -> p w t e", w=2, e=E)
                    nc.vector.tensor_copy(pos[:], m[:, 0])
                    nc.vector.tensor_copy(totals[:], m[:, 1].rearrange("p t e -> p e t")).then_inc(s("m_freed"), 1)
                    dve.wait_ge(s("m_freed"), NTH[r] + 1)
                if kind == "G" and n == 2:
                    dve.wait_ge(s("m_filled"), NTH[r] + 1)
                    a = who * GQ
                    nc.vector.tensor_copy(logits[:, a:a + GQ], ps_m[:, 0:GQ * E].rearrange("p (t e) -> p t e", e=E)).then_inc(s("m_freed"), 1)
                    dve.wait_ge(s("m_freed"), NTH[r] + 1)
                    choose_begin(who)

            def take_output(tiles):
                for j in tiles:
                    if j == 0:
                        dve.wait_ge(s("exp_ready"), 2)
                        link(nc.vector.reciprocal(rinv[:, 0:2], rsum[:, 0:2]))
                    dve.wait_ge(s("output_ready"), tiles[-1] + 1)
                    t = j % GQ
                    nc.vector.scalar_tensor_tensor(o_gated[:, t], ps_o[:, t * P:(t + 1) * P], rinv[:, j:j + 1], mod_b[:, j // TPB, 0],
                                                   ALU.mult, ALU.mult).then_inc(s("o_taken"), 1)

            def residual(j):
                g, t = divmod(j, GQ)
                dve.wait_ge(s("o_taken"), j + 1)
                nc.vector.tensor_tensor(x_sb[:, j], x_sb[:, j], o_gated[:, t], ALU.add).then_inc(s("sum_made"), 1)
                if j + 2 < NT:
                    dve.wait_ge(s("exp_ready"), j + 3)
                    nc.vector.reciprocal(rinv[:, j + 2:j + 3], rsum[:, j + 2:j + 3])
                dve.wait_ge(s("sum_made"), j + 1)
                link(nc.vector.bn_stats(stats2[:, t], x_sb[:, j]))
                if t == 0 and g >= 2:
                    dve.wait_ge(s("h2_ready"), g - 1)
                ins = nc.vector.bn_aggr(mv2[:, g % 2, t], stats2[:, t])
                if t == GQ - 1:
                    link(ins)
                    nc.vector.tensor_scalar(var2[:], mv2[:, g % 2, :, 1], EPS, None, ALU.add).then_inc(s("var2_ready"), 1)

            def choose_begin(g):
                lg = logits[:, g * GQ:(g + 1) * GQ]
                link(nc.vector.tensor_reduce(r_max[:], lg, AX.X, ALU.max))
                nc.vector.tensor_tensor(r_sub[:], lg, r_max[:].rearrange("p (t o) -> p t o", o=1).to_broadcast([P, GQ, E]),
                                        ALU.subtract).then_inc(s("choice_sub"), 1)

            def choose_end(g):
                a, h = g * GQ, g * GQ % HT
                dve.wait_ge(s("choice_exp"), g + 1)
                link(nc.vector.tensor_reduce(r_sum[:], r_exp[:], AX.X, ALU.add))
                link(nc.vector.reciprocal(r_inv[:], r_sum[:]))
                link(nc.vector.tensor_tensor(r_prob[:], r_exp[:], r_inv[:].rearrange("p (t o) -> p t o", o=1).to_broadcast([P, GQ, E]),
                                             ALU.mult))
                for t in range(GQ):
                    ins = nc.vector.max(top_w[:, a + t], r_prob[:, t])
                link(ins)
                for t in range(GQ):
                    ins = nc.vector.max_index(top_i[:, t], top_w[:, a + t], r_prob[:, t])
                link(ins)
                f = top_f[:, h:h + GQ]
                link(nc.vector.tensor_copy(f, top_i[:, :, 0:TOPK]))
                nc.vector.tensor_copy(h2[:, a:a + GQ, D + 1], f[:, :, 1])
                for k in range(TOPK):
                    ins = nc.vector.tensor_tensor(hot[:, k, h:h + GQ], iota_e[:].rearrange("p (o e) -> p o e", o=1).to_broadcast([P, GQ, E]),
                                                  f[:, :, k:k + 1].to_broadcast([P, GQ, E]), ALU.is_equal)
                link(ins)
                nc.vector.tensor_tensor(hot2[:, h:h + GQ], hot[:, 0, h:h + GQ], hot[:, 1, h:h + GQ], ALU.add).then_inc(s("choice_made"), 1)

            def route(half, stage):
                if stage == 0:
                    link(nc.vector.tensor_tensor_scan(upto[:].rearrange("p e t -> p (e t)"), keep[:].rearrange("p e t -> p (e t)"),
                                                      totals[:].rearrange("p e t -> p (e t)"), 0.0, ALU.mult, ALU.add))
                    link(nc.vector.tensor_tensor(cmp_n[:], upto[:, :, HT - 1:HT].to_broadcast([P, E, THR]),
                                            thr[:].rearrange("p (o j) -> p o j", o=1).to_broadcast([P, E, THR]), ALU.is_gt))
                    link(nc.vector.tensor_tensor(upto[:], upto[:], totals[:], ALU.subtract))
                    link(nc.vector.tensor_reduce(n_tiles[:], cmp_n[:], AX.X, ALU.add))
                    link(nc.vector.tensor_tensor_scan(end_t[:], ones[:, 0:E], n_tiles[:], 0.0, ALU.mult, ALU.add))
                    link(nc.vector.tensor_tensor(base_e[:], end_t[:], n_tiles[:], ALU.subtract))
                if stage == 1:
                    link(nc.vector.tensor_scalar(base_e[:], base_e[:], float(P), float(half * TILES * P), ALU.mult, ALU.add))
                    link(nc.vector.tensor_tensor(pos[:], pos[:],
                                                 upto[:].rearrange("p e t -> p t e"), ALU.add))
                    link(nc.vector.tensor_tensor(pos[:], pos[:], base_e[:].rearrange("p (o e) -> p o e", o=1).to_broadcast([P, HT, E]), ALU.add))
                if stage == 2:
                    for k in range(TOPK):
                        ins = nc.vector.tensor_tensor(pos_k[:, k], pos[:], hot[:, k], ALU.mult)
                    link(ins)
                    link(nc.vector.tensor_reduce(slot_f[:], pos_k[:], AX.X, ALU.add))
                    nc.vector.tensor_copy(slot_i[:, half], slot_f[:]).then_inc(s("route_slots"), 1)
                if stage == 3:
                    link(nc.vector.tensor_tensor(cmp_t[:], iota_t[:].rearrange("p (t o) -> p t o", o=1).to_broadcast([P, TILES, E]),
                                                 end_t[:].rearrange("p (o e) -> p o e", o=1).to_broadcast([P, TILES, E]), ALU.is_ge))
                    te = tile_e[:, half * TILES:(half + 1) * TILES]
                    link(nc.vector.tensor_reduce(te, cmp_t[:], AX.X, ALU.add))
                    link(nc.vector.tensor_scalar(te, te, float(E - 1), None, ALU.min))
                    nc.vector.tensor_copy(tile_i[:, half * TILES:(half + 1) * TILES], te).then_inc(s("route_tiles"), 1)
                    dve.wait_ge(s("route_tiles"), half + 1)

            def choices(i):
                for g in range(NG):
                    if logits_step(g) + CHOICE_AFTER.get(g, 3) == i:
                        choose_end(g)

            def attend(i):
                if i < NT:
                    dve.wait_ge(s("scores"), i + 1)
                    nc.vector.tensor_reduce(nmax[:, i:i + 1], ps_s[:, i % 2], AX.X, ALU.max, negate=True).then_inc(s("max_ready"), 1)
                if i == ROUTE0 + 1:
                    choices(i)
                if rounds_of(i, "a"):
                    round_of(rounds_of(i, "a"))
                if i % TPB in (1, 2) and i // TPB + 1 < B:
                    ln1_rows(i // TPB + 1, i % TPB - 1)
                if i == GATE_A_STEP:
                    dve.wait_ge(s("m_freed"), NTH["M", B - 1, 0] + 1)
                    clamp(mod_b[:, :, 0], sgn_b)
                    dve.wait_ge(s("mod_ready"), 2)
                if i > NT:
                    take_output(products_of(i))
                if summed(i - 1) is not None and i < LATE_NORM:
                    ln2_rows(summed(i - 1))
                for j in sums_of(i):
                    residual(j)
                if ln1_of(i):
                    ln1_stats(*ln1_of(i))
                if i == NT - 1:
                    choices(i)
                if i <= NT:
                    take_output(products_of(i))
                if i == ROUTE0 + 2:
                    route(0, 2)
                if summed(i - 1) is not None and i >= LATE_NORM:
                    ln2_rows(summed(i - 1))
                if rounds_of(i, "b"):
                    round_of(rounds_of(i, "b"))
                if i not in (ROUTE0 + 1, NT - 1):
                    choices(i)
                if i == GATE_B_STEP:
                    nc.vector.tensor_scalar(mod_b[:, :, 2], mod_b[:, :, 2], 1.0, None, ALU.add)
                    clamp(mod_b[:, :, 3], sgn_b)
                    dve.wait_ge(s("mod_ready"), 3)
                for stage in {1: (0, 1), 3: (3,)}.get(i - ROUTE0, ()):
                    route(0, stage)

            expert = {}

            def tile(t):
                if t == -2:
                    dve.wait_ge(s("bias_loaded"), 32)
                    dve.wait_ge(s("w1_loaded"), 16)
                if t + 2 < ALL_TILES:
                    n = t + 2
                    v = n % 3
                    dve.wait_ge(s("xT_mm"), n + 1)
                    if t >= 1:
                        dve.wait_ge(s("hid_mm"), t)
                    nc.vector.tensor_copy(xT[:, v], ps_x(n)).then_inc(s("xT_ready"), 1)
                    w = n % NBUF
                    nc.vector.tensor_scalar(dst_f[:, n:n + 1], xs[:, w, D + 1:D + 2], tile_e[:, n:n + 1],
                                            xs[:, w, D:D + 1], ALU.is_equal, ALU.add).then_inc(s("dst_ready"), 1)
                    e = expert[n] = load_expert(dve, n)
                    nc.vector.tensor_copy(w1_t[:, v], w1_sb[:].rearrange("p e h -> p (e h)")[:, bass.ds(e * HID, HID)])
                    if t >= 1:
                        dve.wait_ge(s("gelu_ready"), t)
                    nc.vector.tensor_copy(b1_t[:, v], b1_cols[:, bass.ds(e * HB, HB)]).then_inc(s("tile_weights"), 1)
                if t >= 1:
                    u = (t - 1) % YBUF
                    dve.wait_ge(s("dst_ready"), t)
                    if t - 1 >= YBUF and u % YRUN == 0:
                        dve.wait_ge(s(f"y_out_{u // YRUN}"), 16 * YRUN * ((t - 1) // YBUF))
                    nc.vector.tensor_tensor(dst_i[:, u], dst_f[:, t - 1:t], trash[:, t - 1:t], ALU.min)
                    dve.wait_ge(s("y_mm"), t)
                    nc.vector.tensor_tensor(y_sb[:, u], ps_y(t - 1), b2_bc[:, bass.ds(expert.pop(t - 1) * D, D)],
                                            ALU.add).then_inc(s("y_ready"), 1)

            combines = [0]

            def combine(a, n):
                combines[0] += 1
                dve.wait_ge(s("weighed"), combines[0])
                yc = yy[:, a // CHUNK % 4, a % CHUNK:a % CHUNK + n]
                if n == 1:
                    link(nc.vector.tensor_tensor(yc[:, :, 0:D], yc[:, :, 0:D], yc[:, :, D:2 * D], ALU.add))
                else:
                    for t in range(n):
                        ins = nc.vector.scalar_tensor_tensor(yc[:, t, 0:D], yc[:, t, D:2 * D], top_w[:, a + t, 1:2], yc[:, t, 0:D],
                                                             ALU.mult, ALU.add)
                    link(ins)
                    nc.vector.tensor_tensor(yc[:, :, 0:D], yc[:, :, 0:D], mod_b[:, a // TPB, 3:4].to_broadcast([P, n, D]),
                                            ALU.mult).then_inc(s("gated"), 1)
                    return
                link(nc.vector.tensor_tensor(yc[:, :, 0:D], yc[:, :, 0:D], mod_b[:, a // TPB, 3:4].to_broadcast([P, n, D]), ALU.mult))
                nc.vector.tensor_tensor(x_sb[:, a:a + n], x_sb[:, a:a + n], yc[:, :, 0:D], ALU.add).then_inc(s("combined"), 1)

            def h_low(n):
                dve.wait_ge(s("h_hi_ready"), n + 1)
                nc.vector.tensor_tensor(h_lo[:, n * 512:(n + 1) * 512], h_f[:, n], h_hi[:, n * 512:(n + 1) * 512].bitcast(F32),
                                        ALU.subtract).then_inc(s("h_lo_ready"), 1)

            round_of(("P", 0, 0))
            dve.wait_ge(s("wT_hi_ready"), 1)
            nc.vector.tensor_tensor(wT_lo[:].rearrange("p a b -> p (a b)"), ps_o[:, 0:2 * D],
                                    wT_hi[:].bitcast(F32).rearrange("p a b -> p (a b)"), ALU.subtract).then_inc(s("wT_lo_ready"), 1)
            round_of(("P", 0, 1))
            h_low(0)
            h_low(1)
            dve.wait_ge(s("blank_ready"), 1)
            for b in range(B):
                ins = nc.vector.tensor_scalar(c_rep[:, b], ones[:], c_silu[:, b:b + 1], None, ALU.mult)
            ins.then_inc(s("c_rep_ready"), 1)
            for n in range(2, 8):
                round_of(("P", 0, n))
            for what, n in ORDER:
                if what == "attend":
                    attend(n)
                if what == "tile":
                    tile(n)
                if what == "route":
                    if n == 0:
                        round_of(("R", 1, 0))
                    route(1, n)
                if what == "combine":
                    combine(*n)

        @block.tensor
        def _(pe):
            def product3(o, l_hi, l_lo, r_hi, r_lo, first=True, last=True):
                nc.tensor.matmul(o, l_hi, r_hi, start=first, stop=False)
                nc.tensor.matmul(o, l_hi, r_lo, start=False, stop=False)
                return nc.tensor.matmul(o, l_lo, r_hi, start=False, stop=last)

            pe.wait_ge(s("w_loaded"), 48)
            pe.wait_ge(s("ident_ready"), 1)
            for w in range(3):
                ins = nc.tensor.transpose(ps_o[:, w * D:(w + 1) * D], w_raw[:, w], ident[:])
            ins.then_inc(s("wT_mm"), 1)
            pe.wait_ge(s("wmod_loaded"), 16)
            pe.wait_ge(s("c_silu_ready"), 1)
            for j in range(2):
                ins = nc.tensor.matmul(ps_t[:, 0, j * B:(j + 1) * B], wmod_sb[:, j], c_silu[:], start=True, stop=True)
            ins.then_inc(s("mod_mm"), 1)

            def round_of(r):
                kind, who, n = r
                if NTH[r] >= 8:
                    pe.wait_ge(s("m_freed"), NTH[r])
                bank = bank_of(r)
                if kind == "P" and n < 2:
                    pe.wait_ge(s("z1_ready"), 2 * who + n + 1)
                    for t in range(GQ):
                        ins = nc.tensor.transpose(bank[:, t * P:(t + 1) * P], h2[:, who * TPB + n * GQ + t, 0:D], ident[:])
                if kind == "P" and 2 <= n < 6:
                    if n < 4:
                        pe.wait_ge(s("h_lo_ready"), 2 * who + n - 1)
                    if n == 2:
                        if who == 0:
                            pe.wait_ge(s("wT_lo_ready"), 1)
                            pe.wait_ge(s("mod_ready"), 1)
                    w, col = (n - 2) // 2, (n % 2) * 512
                    ins = product3(bank, wT_hi[:, w], wT_lo[:, w], h_hi[:, col:col + 512], h_lo[:, col:col + 512])
                if kind == "P" and n >= 6:
                    for t in range(GQ):
                        ins = nc.tensor.matmul(bank[:, t * P:(t + 1) * P], h_f[:, n - 6, t * P:(t + 1) * P], wvT, start=True, stop=True)
                if kind == "R":
                    pe.wait_ge(s("choice_made"), (who + 1) * NG // 2)
                    m = hot2[:].rearrange("p t e -> p (t e)")
                    nc.tensor.matmul(ps_m[:, 0:HT * E], before[:], m, start=True, stop=True)
                    ins = nc.tensor.matmul(ps_m[:, HT * E:2 * HT * E], ones[:], m, start=True, stop=True)
                if kind == "M":
                    if who == 0:
                        pe.wait_ge(s("c_rep_ready"), 1)
                    ins = nc.tensor.matmul(ps_m[:], c_rep[:, who], wmod_sb[:, 2:6].rearrange("p a b -> p (a b)"), start=True, stop=True)
                if kind == "G" and n == 1:
                    pe.wait_ge(s("h2_ready"), who + 1)
                    for t in range(GQ):
                        ins = nc.tensor.transpose(ps_m[:, t * P:(t + 1) * P], h2[:, who * GQ + t, 0:D], ident[:])
                if kind == "G" and n == 2:
                    if who == 0:
                        pe.wait_ge(s("router_loaded"), 16)
                    for t in range(GQ):
                        ins = nc.tensor.matmul(ps_m[:, t * E:(t + 1) * E], h2T[:, t * P:(t + 1) * P], wr_sb[:], start=True, stop=True)
                ins.then_inc(s("m_filled"), 1)

            def add_product(j):
                if j % TPB == 0:
                    pe.wait_ge(s("m_freed"), NTH[("P", j // TPB, 7)] + 1)
                if j >= 1:
                    pe.wait_ge(s("o_taken"), j - 1 if j == NT - 3 else j)
                pe.wait_ge(s("copied"), j + 1)
                q = slice(j % GQ * P, (j % GQ + 1) * P)
                for kb in range(TPB):
                    ins = nc.tensor.matmul(ps_o[:, q], pT[:, j // GQ % 2, kb, q], v_sb[:, j // TPB % 2, kb], start=(kb == 0), stop=(kb == TPB - 1))
                ins.then_inc(s("output_ready"), 1)

            def turn(j):
                if not 0 <= j < NT:
                    return
                pe.wait_ge(s("exp_ready"), j + 1)
                if j == 0:
                    pe.wait_ge(s("m_freed"), NTH[("P", 0, 7)] + 1)
                if j >= 1:
                    pe.wait_ge(s("copied"), j)
                for kb in range(TPB):
                    ins = nc.tensor.transpose(ps_t[:, kb], probs[:, j % 2, kb * P:(kb + 1) * P], ident[:])
                ins.then_inc(s("turned"), 1)

            def attend(i):
                if i < NT:
                    b = i // TPB
                    if i >= 2:
                        pe.wait_ge(s("exp_ready"), i - 1)
                    if i % TPB == 0:
                        pe.wait_ge(s("m_freed"), NTH[("P", b, 5)] + 1)
                    q = (i % TPB) * P
                    for half in range(2):
                        ins = product3(ps_s[:, i % 2, half * 512:(half + 1) * 512], q_hi[:, b % 2, q:q + P], q_lo[:, b % 2, q:q + P],
                                       k_hi[:, b % 2, half * 512:(half + 1) * 512], k_lo[:, b % 2, half * 512:(half + 1) * 512])
                    ins.then_inc(s("scores"), 1)
                if rounds_of(i, "a"):
                    round_of(rounds_of(i, "a"))
                if i >= NT - 1:
                    turn(i - 1)
                for j in products_of(i):
                    add_product(j)
                last = rounds_of(i, "b")
                if last and last[0] != "R":
                    round_of(last)
                if i < NT - 1:
                    turn(i - 1)
                if last and last[0] == "R":
                    round_of(last)

            expert = {}

            def tile(t):
                if t + 2 < ALL_TILES:
                    n = t + 2
                    pe.wait_ge(s(f"x_in_{n % NBUF}"), 16 * (n // NBUF + 1))
                    if t >= 0:
                        pe.wait_ge(s("xT_ready"), t + 1)
                    elif t == -2:
                        pe.wait_ge(s("exp_ready"), NT)
                    nc.tensor.transpose(ps_x(n), xs[:, n % NBUF, 0:D], ident[:]).then_inc(s("xT_mm"), 1)
                if t == -1:
                    pe.wait_ge(s("route_tiles"), 1)
                    expert[0] = load_expert(pe, 0)
                if 0 <= t < ALL_TILES:
                    if t == 0:
                        pe.wait_ge(s("w2_loaded"), 16)
                        pe.wait_ge(s("copied"), NT)
                    pe.wait_ge(s("xT_ready"), t + 1)
                    if t >= 2:
                        pe.wait_ge(s("gelu_ready"), t - 1)
                    pe.wait_ge(s("tile_weights"), t + 1)
                    for j in range(HB):
                        ins = nc.tensor.matmul(ps_h(t)[:, j * P:(j + 1) * P], w1_t[:, t % 3, j * P:(j + 1) * P], xT[:, t % 3],
                                               start=True, stop=True)
                    ins.then_inc(s("hid_mm"), 1)
                    if t + 1 < ALL_TILES:
                        if (t + 1) % TILES == 0:
                            pe.wait_ge(s("route_tiles"), (t + 1) // TILES + 1)
                        expert[t + 1] = load_expert(pe, t + 1)
                if t >= 1:
                    pe.wait_ge(s("gelu_ready"), t)
                    if t >= 3:
                        pe.wait_ge(s("y_ready"), t - 2)
                    w = w2_sb[:].rearrange("p e j d -> p (e j d)")
                    at = expert.pop(t - 1) * (HB * D)
                    for j in range(HB):
                        ins = nc.tensor.matmul(ps_y(t - 1), gT[:, (t - 1) % 2, j * P:(j + 1) * P],
                                               w[:, bass.ds(at + j * D, D)], start=(j == 0), stop=(j == HB - 1))
                    ins.then_inc(s("y_mm"), 1)

            for n in range(8):
                round_of(("P", 0, n))
            for what, n in ORDER:
                if what == "attend":
                    attend(n)
                if what == "tile":
                    tile(n)
                if what == "route" and n == 0:
                    round_of(("R", 1, 0))


_INS = ['L0_attn_x', 'L0_attn_Wq', 'L0_attn_bq', 'L0_attn_Wk', 'L0_attn_bk', 'L0_attn_Wv', 'L0_attn_bv',
        'L0_ffn_w_router', 'L0_ffn_w1', 'L0_ffn_b1', 'L0_ffn_w2', 'L0_ffn_b2', 'L0_c', 'L0_wmod']


def kernel(**inputs):
    import numpy as _np
    import concourse.bacc as _bacc
    from concourse import mybir as _mybir
    from concourse.bass_utils import run_bass_kernel_spmd as _run

    nc = _bacc.Bacc("TRN2", target_bir_lowering=False, num_devices=1)
    arrays, args = {}, []
    for name in _INS:
        a = _np.ascontiguousarray(inputs[name])
        arrays[f"in_{name}_dram"] = a
        args.append(nc.dram_tensor(f"in_{name}_dram", a.shape, _mybir.dt.from_np(a.dtype), kind="ExternalInput").ap())
    args.append(nc.dram_tensor("out_dram", (B, SEQ, D), F32, kind="ExternalOutput").ap())
    build(nc, *args)
    r = _run(nc, [arrays], core_ids=[0])
    return r.results[0]["out_dram"]
```
